# Optimizing a Trainium2 kernel written in Bass

```python
import numpy as np
import jax
import jax.numpy as jnp

def _softmax(x, axis=-1):
    return jax.nn.softmax(x, axis=axis)

def _gelu(x):
    return jax.nn.gelu(x, approximate=True)

def _silu(x):
    return jax.nn.silu(x)

def _sigmoid(x):
    return jax.nn.sigmoid(x)

def _layernorm(x, axis=-1, eps=1e-05):
    m = jnp.mean(x, axis=axis, keepdims=True)
    v = jnp.var(x, axis=axis, keepdims=True)
    return (x - m) / jnp.sqrt(v + eps)

def _scatter_add(tgt, idx, src, axis=0):
    return tgt.at[idx].add(src)

def _segment_sum(src, seg, n):
    return jax.ops.segment_sum(src, seg, n)
kernel_name = 'mk_seq_postln_d1_jaxref_r8_12b81b'

def setup_inputs(seed: int=0):
    np.random.seed(seed)
    _w = jnp.asarray

    def _L0_attn_setup():
        import jax, jax.numpy as jnp
        import numpy as np
        _J6 = jnp.array([[0, 0, 0, 0, 0, 1], [0, 0, 0, 0, -1, 0], [0, 0, 0, 1, 0, 0], [0, 0, 1, 0, 0, 0], [0, -1, 0, 0, 0, 0], [1, 0, 0, 0, 0, 0]], dtype=jnp.float32)
        _PAIRS = [(0, 1), (0, 2), (0, 3), (1, 2), (1, 3), (2, 3)]
        _H = 16
        _SCALE = 6.0 ** (-0.5)

        def _plucker_lines(p1, p2):
            parts = [p1[..., i] * p2[..., j] - p1[..., j] * p2[..., i] for i, j in _PAIRS]
            lines = jnp.stack(parts, axis=-1)
            n = jnp.linalg.norm(lines, axis=-1, keepdims=True)
            return lines / jnp.maximum(n, 1e-12)
        key = jax.random.key(seed)
        ks = jax.random.split(key, 9)
        B, T, D, H = (2, 256, 128, _H)
        std = 0.02
        return {'x': jax.random.normal(ks[0], (B, T, D), jnp.float32), 'W1_q': jax.random.normal(ks[1], (4 * H, 2 * D), jnp.float32) * std, 'W2_q': jax.random.normal(ks[2], (4 * H, 2 * D), jnp.float32) * std, 'W1_k': jax.random.normal(ks[3], (4 * H, D), jnp.float32) * std, 'W2_k': jax.random.normal(ks[4], (4 * H, D), jnp.float32) * std, 'Wv': jax.random.normal(ks[5], (D, D), jnp.float32) * std, 'bv': jnp.zeros((D,), jnp.float32), 'Wo': jax.random.normal(ks[6], (D, D), jnp.float32) * std, 'bo': jnp.zeros((D,), jnp.float32)}
    _L0_attn_in = _L0_attn_setup()

    def _L0_ffn_setup():
        import jax, jax.numpy as jnp
        import numpy as np
        B, S, H, I, E_ROUTED, TOP_K = (8, 256, 128, 256, 8, 2)

        def _expert(x, Wg, Wu, Wd):
            return jax.nn.silu(x @ Wg.T) * (x @ Wu.T) @ Wd.T
        key = jax.random.key(seed)
        ks = jax.random.split(key, 9)
        s = 0.02
        return {'x': jax.random.normal(ks[0], (B, S, H), dtype=jnp.float32), 'Wg_s': jax.random.normal(ks[1], (I, H), dtype=jnp.float32) * s, 'Wu_s': jax.random.normal(ks[2], (I, H), dtype=jnp.float32) * s, 'Wd_s': jax.random.normal(ks[3], (H, I), dtype=jnp.float32) * s, 'Wg': jax.random.normal(ks[4], (E_ROUTED, I, H), dtype=jnp.float32) * s, 'Wu': jax.random.normal(ks[5], (E_ROUTED, I, H), dtype=jnp.float32) * s, 'Wd': jax.random.normal(ks[6], (E_ROUTED, H, I), dtype=jnp.float32) * s, 'Wr': jax.random.normal(ks[7], (E_ROUTED, H), dtype=jnp.float32) * s, 'rb': jnp.zeros((E_ROUTED,), dtype=jnp.float32)}
    _L0_ffn_in = _L0_ffn_setup()
    _d = {'L0_attn_x': _L0_attn_in['x'], 'L0_attn_W1_q': _L0_attn_in['W1_q'], 'L0_attn_W2_q': _L0_attn_in['W2_q'], 'L0_attn_W1_k': _L0_attn_in['W1_k'], 'L0_attn_W2_k': _L0_attn_in['W2_k'], 'L0_attn_Wv': _L0_attn_in['Wv'], 'L0_attn_bv': _L0_attn_in['bv'], 'L0_attn_Wo': _L0_attn_in['Wo'], 'L0_attn_bo': _L0_attn_in['bo'], 'L0_ffn_Wg_s': _L0_ffn_in['Wg_s'], 'L0_ffn_Wu_s': _L0_ffn_in['Wu_s'], 'L0_ffn_Wd_s': _L0_ffn_in['Wd_s'], 'L0_ffn_Wg': _L0_ffn_in['Wg'], 'L0_ffn_Wu': _L0_ffn_in['Wu'], 'L0_ffn_Wd': _L0_ffn_in['Wd'], 'L0_ffn_Wr': _L0_ffn_in['Wr'], 'L0_ffn_rb': _L0_ffn_in['rb']}
    _x0 = _d['L0_attn_x']
    _d['L0_attn_x'] = jax.random.normal(jax.random.fold_in(jax.random.key(seed), 1), (16, 512, 128), dtype=_x0.dtype)
    del _x0
    return _d

def reference(L0_attn_x, L0_attn_W1_q, L0_attn_W2_q, L0_attn_W1_k, L0_attn_W2_k, L0_attn_Wv, L0_attn_bv, L0_attn_Wo, L0_attn_bo, L0_ffn_Wg_s, L0_ffn_Wu_s, L0_ffn_Wd_s, L0_ffn_Wg, L0_ffn_Wu, L0_ffn_Wd, L0_ffn_Wr, L0_ffn_rb):

    def _L0_attn_ref(x, W1_q, W2_q, W1_k, W2_k, Wv, bv, Wo, bo):
        import jax, jax.numpy as jnp
        import numpy as np
        _J6 = jnp.array([[0, 0, 0, 0, 0, 1], [0, 0, 0, 0, -1, 0], [0, 0, 0, 1, 0, 0], [0, 0, 1, 0, 0, 0], [0, -1, 0, 0, 0, 0], [1, 0, 0, 0, 0, 0]], dtype=jnp.float32)
        _PAIRS = [(0, 1), (0, 2), (0, 3), (1, 2), (1, 3), (2, 3)]
        _H = 16
        _SCALE = 6.0 ** (-0.5)

        def _plucker_lines(p1, p2):
            parts = [p1[..., i] * p2[..., j] - p1[..., j] * p2[..., i] for i, j in _PAIRS]
            lines = jnp.stack(parts, axis=-1)
            n = jnp.linalg.norm(lines, axis=-1, keepdims=True)
            return lines / jnp.maximum(n, 1e-12)
        B, T, D = x.shape
        H = _H
        dh = D // H
        x_prev = jnp.pad(x[:, :-1, :], ((0, 0), (1, 0), (0, 0)))
        bg = jnp.concatenate([x, x_prev], axis=-1)
        q1 = (bg @ W1_q.T).reshape(B, T, H, 4)
        q2 = (bg @ W2_q.T).reshape(B, T, H, 4)
        k1 = (x @ W1_k.T).reshape(B, T, H, 4)
        k2 = (x @ W2_k.T).reshape(B, T, H, 4)
        q = _plucker_lines(q1, q2).transpose(0, 2, 1, 3)
        k = _plucker_lines(k1, k2).transpose(0, 2, 1, 3)
        Jk = k @ _J6.T
        logits = jnp.einsum('bhtc,bhsc->bhts', q, Jk) * _SCALE
        causal = jnp.tril(jnp.ones((T, T), dtype=bool))
        logits = jnp.where(causal[None, None], logits, -jnp.inf)
        attn = jax.nn.softmax(logits, axis=-1)
        v = (x @ Wv.T + bv).reshape(B, T, H, dh).transpose(0, 2, 1, 3)
        o = jnp.einsum('bhts,bhsd->bhtd', attn, v)
        o = o.transpose(0, 2, 1, 3).reshape(B, T, D)
        return o @ Wo.T + bo

    def _L0_ffn_ref(x, Wg_s, Wu_s, Wd_s, Wg, Wu, Wd, Wr, rb):
        import jax, jax.numpy as jnp
        import numpy as np
        B, S, H, I, E_ROUTED, TOP_K = (8, 256, 128, 256, 8, 2)

        def _expert(x, Wg, Wu, Wd):
            return jax.nn.silu(x @ Wg.T) * (x @ Wu.T) @ Wd.T
        shared = _expert(x, Wg_s, Wu_s, Wd_s)
        logits = jnp.einsum('bsh,eh->bse', x, Wr) + rb
        probs = jax.nn.sigmoid(logits)
        scores, idx = jax.lax.top_k(probs, TOP_K)
        cw = (jax.nn.one_hot(idx, E_ROUTED, dtype=x.dtype) * scores[..., None]).sum(-2)
        out = shared
        for e in range(E_ROUTED):
            out = out + cw[..., e:e + 1] * _expert(x, Wg[e], Wu[e], Wd[e])
        return out
    x = L0_attn_x
    x = _layernorm(x + _L0_attn_ref(x, L0_attn_W1_q, L0_attn_W2_q, L0_attn_W1_k, L0_attn_W2_k, L0_attn_Wv, L0_attn_bv, L0_attn_Wo, L0_attn_bo), axis=-1)
    x = _layernorm(x + _L0_ffn_ref(x, L0_ffn_Wg_s, L0_ffn_Wu_s, L0_ffn_Wd_s, L0_ffn_Wg, L0_ffn_Wu, L0_ffn_Wd, L0_ffn_Wr, L0_ffn_rb), axis=-1)
    return x

_drawn_inputs = setup_inputs


def setup_inputs(seed=0):
    import zlib

    import numpy as np

    out = dict(_drawn_inputs(seed))
    spreads = {'L0_attn_bv': (0.0, 0.352), 'L0_attn_bo': (0.0, 0.1), 'L0_ffn_rb': (0.0, 0.8)}
    factors = {'L0_attn_W1_q': 8.0,
     'L0_attn_W2_q': 8.0,
     'L0_attn_W1_k': 8.0,
     'L0_attn_W2_k': 8.0,
     'L0_attn_Wv': 8.0,
     'L0_ffn_Wg_s': 6.799,
     'L0_ffn_Wu_s': 6.698,
     'L0_ffn_Wd_s': 6.644,
     'L0_ffn_Wg': 8.0,
     'L0_ffn_Wu': 8.0,
     'L0_ffn_Wd': 8.0,
     'L0_ffn_Wr': 8.0}
    for name, (base, spread) in spreads.items():
        noise = np.random.default_rng([zlib.crc32(name.encode()), seed]).standard_normal(out[name].shape)
        drawn = base * np.exp(spread * noise) if base else spread * noise
        out[name] = jnp.asarray(drawn.astype(out[name].dtype))
    for name, factor in factors.items():
        out[name] = (out[name] * factor).astype(out[name].dtype)
    return out
```

```python
import concourse.bass as bass
from concourse import mybir
from contextlib import ExitStack

FP32 = mybir.dt.float32
FP16 = mybir.dt.float16
I32 = mybir.dt.int32
ALU = mybir.AluOpType
ACT = mybir.ActivationFunctionType
AX = mybir.AxisListType

P = 128
T = 512
NT = T // P
H = 16
DH = P // H
HP = H // 4
LINE = 6
FEAT = 32
HH = 2 * H
SPLIT_UP = 1024.0
SCALE = 6.0 ** -0.5
NE = 8
FF = 256
EPS = 1e-5

CHUNK = 1024
NCHUNK = 5
PIECES = {
    (0, 0): (0, 0), (0, 3): (0, 512), (0, 1): (0, 640),
    (1, 0): (1, 0), (1, 3): (1, 512), (1, 1): (1, 640),
    (0, 2): (2, 0), (2, 0): (2, 512), (1, 2): (2, 256),
    (2, 3): (3, 0), (2, 1): (3, 128), (3, 0): (3, 512),
    (2, 2): (4, 512), (3, 3): (4, 0), (3, 1): (4, 128), (3, 2): (4, 768),
}
BANK_MATE = {(1, 2): (0, 2), (3, 2): (2, 2)}
SQUARES = {
    0: [(0, 1, 128), (512, 2, 128)],
    1: [(0, 1, 128), (512, 2, 128)],
    2: [(0, 3, 256)],
    3: [(0, 2, 128), (512, 1, 128)],
    4: [(0, 2, 128), (512, 2, 256)],
}


def spread(ap, dim, n):
    shape = list(ap.shape)
    shape[dim] = n
    return ap.broadcast_to(shape)


def block_program(nc, x, W1_q, W2_q, W1_k, W2_k, Wv, bv, Wo, bo, Wg_s, Wu_s, Wd_s, Wg, Wu, Wd, Wr, rb, out):
    NB = x.shape[0]
    ctx = ExitStack()
    with ctx:
        def sb(name, shape, dt=FP32):
            return ctx.enter_context(nc.sbuf_tensor(name, shape, dt))

        def pb(name, shape, dt=FP32):
            return ctx.enter_context(nc.psum_tensor(name, shape, dt))

        def sem(name):
            return ctx.enter_context(nc.semaphore(name))

        phase1 = ExitStack()

        def sb1(name, shape, dt=FP32):
            return phase1.enter_context(nc.sbuf_tensor(name, shape, dt))

        ident = sb("ident", [P, P])
        ident16 = sb("ident16", [P, P], FP16)
        minus_half = sb("minus_half", [P, 4])
        w_nat = sb1("w_nat", [P, 8, P])
        w_allT = sb1("w_allT", [P, 3 * P])
        w_prevT = sb1("w_prevT", [P, P])
        w_oT = sb1("w_oT", [P, P])
        bv_col = sb1("bv_col", [P, 1])
        bv_cols = sb1("bv_cols", [P, P])
        bo_bc = sb1("bo_bc", [P, P])
        x_in = sb1("x_in", [P, 2, NT, P])
        xres = sb1("xres", [P, 2, NT, P])
        xT = sb1("xT", [P, T + 1])
        p12 = sb1("p12", [P, 2, 2, NT, H, 4])
        v_aug = sb1("v_aug", [P, 2, NT, H, 32])
        prodA = sb1("prodA", [P, NT * HH, LINE])
        prodB = sb1("prodB", [P, NT * HH, LINE])
        nrm = sb1("nrm", [P, NT * HH])
        nhalf = sb1("nhalf", [P, NT * HH])
        rs_a = sb1("rs_a", [P, NT * HH])
        rs_b = sb1("rs_b", [P, NT * HH])
        feat = sb1("feat", [P, NT * HH, FEAT], FP16)
        qkT = sb1("qkT", [P, 2, HP, 2, T], FP16)
        probs = sb1("probs", [P, 2, NCHUNK, CHUNK])
        oT_raw = sb1("oT_raw", [P, HP, T])
        rden = sb1("rden", [P, NT, H])
        o_tok = sb1("o_tok", [P, NT, P])
        oT = sb1("oT", [P, T])
        ysum = sb1("ysum", [P, NT, P])
        stats = sb1("stats", [P, NT, 6])
        meanvar = sb1("meanvar", [P, NT, 2])
        vareps = sb1("vareps", [P, NT])
        rstd = sb1("rstd", [P, NT])
        x1 = sb1("x1", [P, 2, NT, P])
        x1_dram = nc.dram_tensor("x1_scratch", (NB, T, P), FP32).ap()

        S = [pb(f"S{i}", [P, CHUNK]) for i in range(2)]
        O = [pb(f"O{i}", [P, T]) for i in range(2)]
        W0 = pb("W0", [P, T])
        W1 = pb("W1", [P, T])
        W = [W0, W1]

        wts_in = sem("wts_in"); consts = sem("consts"); xin_in = [sem("xin_in0"), sem("xin_in1")]
        wT_full = sem("wT_full"); wT_read = sem("wT_read")
        xT_full = sem("xT_full"); xT_read = sem("xT_read")
        proj_full = sem("proj_full"); proj_read = sem("proj_read")
        prodB_done = sem("prodB_done"); prodB_read = sem("prodB_read")
        feat_done = sem("feat_done"); featT_full = sem("featT_full"); featT_read = sem("featT_read")
        s_full = sem("s_full"); s_exp = sem("s_exp"); masked = sem("masked"); pv_done = sem("pv_done")
        o_read = sem("o_read")
        outT_full = sem("outT_full"); outT_read = sem("outT_read")
        oT_full = sem("oT_full"); oT_read = sem("oT_read")
        y_full = sem("y_full"); y_read = sem("y_read")
        var_done = sem("var_done"); rstd_done = sem("rstd_done")
        x1_done = sem("x1_done"); x1_out = [sem("x1_out0"), sem("x1_out1")]
        dve_step = sem("dve_step"); pool_step = sem("pool_step")
        xres_done = sem("xres_done"); parted = sem("parted"); mate_done = sem("mate_done"); bv_spread = sem("bv_spread")

        loads = [
            (w_nat[0:64, 0, :], W1_q[:, 0:P]), (w_nat[64:128, 0, :], W1_k),
            (w_nat[0:64, 1, :], W2_q[:, 0:P]), (w_nat[64:128, 1, :], W2_k),
            (w_nat[:, 2, :], Wv), (w_nat[0:64, 3, :], W1_q[:, P:2 * P]), (w_nat[64:128, 3, :], W2_q[:, P:2 * P]),
            (w_nat[:, 4, :], Wo),
            (bv_col[:, :], bv.rearrange("(p o) -> p o", o=1)),
            (bo_bc[:, :], bo.partition_broadcast(P)),
        ]

        def over_batches(eng, body):
            body(0, 0, True, False)
            with eng.Fori(0, NB // 2 - 1) as i:
                body(2 * i + 1, 1, False, False)
                body(2 * i + 2, 0, False, False)
            body(NB - 1, 1, False, True)

        def products(dst, many, one):
            d = dst[:, :, :].rearrange("p (s h) l -> p s h l", s=2)
            q_many, k_many = (p12[:, many, s].rearrange("p t h c -> p (t h) c") for s in range(2))
            q_one, k_one = (p12[:, one, s].rearrange("p t h c -> p (t h) c") for s in range(2))
            for i, l0, n in ((0, 0, 3), (1, 3, 2), (2, 5, 1)):
                yield d[:, 0, :, l0:l0 + n], q_many[:, :, i + 1:4], spread(q_one[:, :, i:i + 1], 2, n)
            for j, l0, n in ((1, 0, 1), (2, 1, 2), (3, 3, 3)):
                yield d[:, 1, :, l0:l0 + n], spread(k_many[:, :, j:j + 1], 2, n), k_one[:, :, 0:n]

        block_scope = ExitStack()
        block = block_scope.enter_context(nc.Block())

        @block.sync
        def _(sp):
            for dst, src in loads:
                sp.dma_start(dst, src).then_inc(wts_in, 16)
            for par in range(2):
                sp.sem_inc(x1_out[par], 16)

            def body(b, par, first, last):
                if not first:
                    sp.wait_ge(x1_done, b)
                    sp.dma_start(x1_dram[bass.ds(b - 1, 1)].rearrange("a (t p) d -> p (a t) d", p=P), x1[:, 1 - par])\
                        .then_inc(x1_out[1 - par], 16)
            over_batches(sp, body)
            sp.wait_ge(x1_done, NB)
            sp.dma_start(x1_dram[NB - 1].rearrange("(t p) d -> p t d", p=P), x1[:, 1]).then_inc(x1_out[1], 16)
            for par in range(2):
                sp.wait_ge(x1_out[par], 16 * NB // 2 + 16)

        @block.gpsimd
        def _(pool):
            steps = [0]

            def then_wait(ins):
                steps[0] += 1
                ins.then_inc(pool_step, 1)
                pool.wait_ge(pool_step, steps[0])
            pool.memset(ident[:, :], 0.0).then_inc(pool_step, 1)
            pool.memset(ident16[:, :], 0.0).then_inc(pool_step, 1)
            pool.wait_ge(pool_step, 2)
            for m in (ident, ident16):
                pool.affine_select(out=m[:, :], in_=m[:, :], compare_op=ALU.not_equal, fill=1.0, base=0,
                                   pattern=[[-1, P]], channel_multiplier=1).then_inc(consts, 1)
            pool.memset(minus_half[:, :], -0.5).then_inc(consts, 1)
            pool.memset(xT[:, 0:1], 0.0).then_inc(consts, 1)
            pool.memset(feat[:, :, :], 0.0).then_inc(consts, 1)
            pool.memset(v_aug[:, :, :, :, :], 0.0).then_inc(pool_step, 1)
            pool.wait_ge(pool_step, 3)
            for par in range(2):
                pool.memset(v_aug[:, par, :, :, DH:DH + 1].rearrange("p t h o -> p (t h) o"), 1.0)\
                    .then_inc(consts, 1)

            def line_products(c):
                pool.wait_ge(proj_read, NT * (c + 1))
                pool.wait_ge(prodB_read, c)
                for dst, many, one in products(prodB, 0, 1):
                    pool.tensor_tensor(dst, many, one, ALU.mult).then_inc(prodB_done, 1)

            def inv_std(c):
                pool.wait_ge(var_done, c + 1)
                pool.tensor_tensor(rstd[:, :], vareps[:, :], minus_half[:, :], ALU.pow).then_inc(rstd_done, 1)

            def mask(b, g):
                for c in range(NCHUNK):
                    pool.wait_ge(s_exp, NCHUNK * HP * b + NCHUNK * g + c + 1)
                    pool.sem_inc(parted, 1)
                    for col, n, step in SQUARES[c]:
                        v = probs[:, g % 2, c, col:col + (n - 1) * step + P] if step == P or n == 1 else None
                        if v is None:
                            v = probs[:, g % 2, c, col:col + n * step].rearrange("p (n k) -> p n k", n=n)[:, :, 0:P]
                        else:
                            v = v.rearrange("p (n k) -> p n k", n=n)
                        pool.affine_select(out=v, in_=v, compare_op=ALU.is_ge, fill=0.0, base=0,
                                           pattern=[[0, n], [1, P]], channel_multiplier=-1).then_inc(masked, 1)
            line_products(0)

            def body(b, par, first, last):
                mask(b, 0)
                mask(b, 1)
                if not last:
                    line_products(b + 1)
                mask(b, 2)
                if not first:
                    inv_std(b - 1)
                mask(b, 3)
            over_batches(pool, body)
            inv_std(NB - 1)
        NMASK = sum(len(v) for v in SQUARES.values())
        NPROD = 6

        @block.tensor
        def _(pe):
            pe.wait_ge(consts, 7)
            pe.wait_ge(wts_in, 16 * len(loads))
            for j in range(5):
                if j >= 2:
                    pe.wait_ge(wT_read, j - 1)
                pe.transpose(W[j % 2][:, 0:P], w_nat[:, j, :], ident[:, :]).then_inc(wT_full, 1)

            def transpose_x(c, par):
                pe.wait_ge(xin_in[par], 16 * (c // 2 + 1) if isinstance(c, int) else 16 * ((c - par) // 2 + 1))
                for t in range(NT):
                    mm = pe.transpose(W0[:, t * P:(t + 1) * P], x_in[:, par, t, :], ident[:, :])
                mm.then_inc(xT_full, 1)

            def project(c, t):
                w = W[(t + 1) % 2]
                if t == 0:
                    pe.wait_ge(xT_read, c + 1)
                if t >= 2:
                    pe.wait_ge(proj_read, NT * c + t - 1)
                pe.matmul(w[:, 0:3 * P], xT[:, 1 + t * P:1 + (t + 1) * P], w_allT[:, :], start=True, stop=False,
                          skip_group_check=True)
                pe.matmul(w[:, 0:2 * P].rearrange("p (a n) -> p a n", a=2)[:, :, 0:H * 4], xT[:, t * P:(t + 1) * P],
                          w_prevT[:, :].rearrange("p (a n) -> p a n", a=2), start=False, stop=True,
                          skip_group_check=True)\
                    .then_inc(proj_full, 1)

            def transpose_feat(c, g):
                w = W[(g + 1) % 2][:, :].bitcast(FP16).rearrange("p (s n) -> p s n", s=2)
                if g == 0:
                    pe.wait_ge(feat_done, c + 1)
                else:
                    pe.wait_ge(featT_read, HP * c + g - 1)
                for s in range(2):
                    for t in range(NT):
                        first = s * NT * H + t * H + 4 * g
                        mm = pe.transpose(w[:, s, t * P:(t + 1) * P],
                                          feat[:, first:first + 4, :].rearrange("p h f -> p (h f)"), ident16[:, :])
                mm.then_inc(featT_full, 1)

            MATES = len(BANK_MATE)
            mates = [0]

            def scores(b, par, g, chunks):
                if chunks[0] == 0:
                    mates[0] = 0
                for c in chunks:
                    n = NCHUNK * HP * b + NCHUNK * g + c
                    if not (isinstance(n, int) and n < 2):
                        pe.wait_ge(s_exp, n - 1)
                    if c == 0:
                        pe.wait_ge(featT_read, HP * b + g + 1)
                    for (j, kb), (cc, col) in PIECES.items():
                        if cc == c:
                            q = qkT[32 * j:32 * j + 32, par, g, 0, kb * P:T]
                            k = qkT[32 * j:32 * j + 32, par, g, 1, kb * P:(kb + 1) * P]
                            if (j, kb) in BANK_MATE:
                                mates[0] += 1
                                pe.wait_ge(mate_done, MATES * (HP * b + g) + mates[0])
                            mm = pe.matmul(S[(g + c) % 2][:, col:col + T - kb * P], k, q, start=True, stop=True)
                            if (j, kb) in BANK_MATE.values():
                                mm.then_inc(mate_done, 1)
                    mm.then_inc(s_full, 1)

            def weigh(b, par, g):
                pe.wait_ge(masked, NMASK * (HP * b + g + 1))
                n = HP * b + g
                if not (isinstance(n, int) and n < 2):
                    pe.wait_ge(o_read, n - 1)
                for kb in range(NT):
                    for j in range(4):
                        c, col = PIECES[(j, kb)]
                        mm = pe.matmul(O[g % 2][32 * j:32 * j + 32, kb * P:T], v_aug[:, par, kb, 4 * g + j, :],
                                       probs[:, g % 2, c, col:col + T - kb * P], start=(kb == 0), stop=(kb == NT - 1),
                                       skip_group_check=True)
                mm.then_inc(pv_done, 1)

            def transpose_out(c, t, after):
                if t == 0:
                    pe.wait_ge(o_read, HP * (c + 1))
                    if after:
                        pe.wait_ge(proj_read, NT * (c + 3))
                    else:
                        pe.wait_ge(featT_read, HP * NB)
                        pe.wait_ge(y_read, c)
                elif t > 1:
                    pe.wait_ge(outT_read, NT * c + t - 1)
                for g in range(HP):
                    mm = pe.transpose(W[(t + 1) % 2][:, g * P:(g + 1) * P], oT_raw[:, g, t * P:(t + 1) * P], ident[:, :])
                mm.then_inc(outT_full, 1)

            def transpose_o(c):
                pe.wait_ge(outT_read, NT * (c + 1))
                for t in range(NT):
                    mm = pe.transpose(W1[:, t * P:(t + 1) * P], o_tok[:, t, :], ident[:, :])
                mm.then_inc(oT_full, 1)

            def project_out(c):
                pe.wait_ge(oT_read, c + 1)
                for t in range(NT):
                    mm = pe.matmul(W0[:, t * P:(t + 1) * P], oT[:, t * P:(t + 1) * P], w_oT[:, :], start=True, stop=True)
                mm.then_inc(y_full, 1)

            pe.wait_ge(wT_read, 5)
            pe.wait_ge(bv_spread, 1)
            pe.matmul(W1[:, 0:P], bv_cols[:, :], w_oT[:, :], start=True, stop=True).then_inc(wT_full, 1)
            pe.wait_ge(wT_read, 6)
            transpose_x(0, 0)
            for t in range(NT):
                project(0, t)
            pe.wait_ge(proj_read, NT)
            for g in range(HP):
                transpose_feat(0, g)

            def body(b, par, first, last):
                scores(b, par, 0, (0, 1))
                if not first:
                    weigh(b - 1, 1 - par, 3)
                if not last:
                    pe.wait_ge(featT_read, HP * (b + 1))
                    transpose_x(b + 1, 1 - par)
                scores(b, par, 0, (2, 3, 4))
                if not last:
                    project(b + 1, 0)
                    project(b + 1, 1)
                scores(b, par, 1, (0, 1))
                weigh(b, par, 0)
                scores(b, par, 1, (2, 3, 4))
                if not last:
                    project(b + 1, 2)
                    project(b + 1, 3)
                if not first:
                    for t in range(NT):
                        transpose_out(b - 1, t, not last)
                scores(b, par, 2, (0, 1))
                weigh(b, par, 1)
                scores(b, par, 2, (2, 3, 4))
                if not first:
                    transpose_o(b - 1)
                scores(b, par, 3, (0, 1))
                weigh(b, par, 2)
                if not first:
                    project_out(b - 1)
                scores(b, par, 3, (2, 3, 4))
                if not last:
                    if not first:
                        pe.wait_ge(y_read, b)
                    else:
                        pe.wait_ge(proj_read, 2 * NT)
                    for g in range(HP):
                        transpose_feat(b + 1, g)
            over_batches(pe, body)
            weigh(NB - 1, 1, 3)
            for t in range(NT):
                transpose_out(NB - 1, t, False)
            transpose_o(NB - 1)
            project_out(NB - 1)

        @block.scalar
        def _(act):
            def copy_projection(c, par, t):
                act.wait_ge(proj_full, NT * c + t + 1)
                if t == 0:
                    act.wait_ge(prodB_done, NPROD * c)
                    act.wait_ge(prodB_read, c)
                    if not (isinstance(c, int) and c < 2):
                        act.wait_ge(pv_done, HP * (c - 1))
                act.copy(p12[:, :, :, t].rearrange("p a s h c -> p (a s) (h c)"),
                         W[(t + 1) % 2][:, 0:2 * P].rearrange("p (a n) -> p a n", a=4))
                act.copy(v_aug[:, par, t, :, 0:DH], W[(t + 1) % 2][:, 2 * P:3 * P].rearrange("p (h d) -> p h d", d=DH))\
                    .then_inc(proj_read, 1)

            def exps(b, g, chunks):
                for c in chunks:
                    n = HP * b + g
                    act.wait_ge(s_full, NCHUNK * n + c + 1)
                    if c == 0 and not (isinstance(n, int) and n < 2):
                        act.wait_ge(pv_done, n - 1)
                    act.activation(probs[:, g % 2, c, :], S[(g + c) % 2][:, :], ACT.Exp,
                                   scale=-SCALE / SPLIT_UP ** 2).then_inc(s_exp, 1)

            def copy_out(b, g):
                act.wait_ge(pv_done, HP * b + g + 1)
                if g == 0:
                    act.wait_ge(outT_full, NT * b)
                act.copy(oT_raw[:, g, :], O[g % 2][:, :]).then_inc(o_read, 1)

            def copy_oT(c):
                act.wait_ge(oT_full, c + 1)
                act.wait_ge(y_full, c)
                act.copy(oT[:, :], W1[:, :]).then_inc(oT_read, 1)

            def load_x(c, par):
                act.wait_ge(xres_done, c - 1) if not (isinstance(c, int) and c < 2) else None
                act.dma_start(x_in[:, par], x[bass.ds(c, 1)].rearrange("a (t p) d -> p (a t) d", p=P))\
                    .then_inc(xin_in[par], 16)

            load_x(0, 0)
            load_x(1, 1)
            for t in range(NT):
                copy_projection(0, 0, t)

            def body(b, par, first, last):
                if not first and not last:
                    load_x(b + 1, 1 - par)
                exps(b, 0, (0, 1, 2))
                if not first:
                    copy_out(b - 1, 3)
                exps(b, 0, (3, 4))
                if not last:
                    copy_projection(b + 1, 1 - par, 0)
                    copy_projection(b + 1, 1 - par, 1)
                exps(b, 1, (0, 1, 2))
                if first:
                    copy_out(b, 0)
                exps(b, 1, (3, 4))
                if not last:
                    copy_projection(b + 1, 1 - par, 2)
                    copy_projection(b + 1, 1 - par, 3)
                exps(b, 2, (0,))
                if not first:
                    copy_out(b, 0)
                exps(b, 2, (1, 2))
                copy_out(b, 1)
                exps(b, 2, (3, 4))
                if not first:
                    copy_oT(b - 1)
                exps(b, 3, (0, 1, 2))
                copy_out(b, 2)
                exps(b, 3, (3, 4))
            over_batches(act, body)
            copy_out(NB - 1, 3)
            copy_oT(NB - 1)

        @block.vector
        def _(dve):
            base, count = [0], [0]

            def chain(ins):
                ins.then_inc(dve_step, 1)
                count[0] += 1
                dve.wait_ge(dve_step, base[0] + count[0])

            dve.wait_ge(consts, 7)
            for j in range(5):
                dve.wait_ge(wT_full, j + 1)
                src = W[j % 2][:, 0:P]
                if j == 2:
                    ins = dve.tensor_copy(w_allT[:, 2 * P:3 * P], src)
                elif j == 4:
                    ins = dve.tensor_copy(w_oT[:, :], src)
                else:
                    src = src.rearrange("p (s h c) -> p s h c", s=2, c=4)
                    dst = (w_allT[:, j * P:(j + 1) * P] if j < 2 else w_prevT[:, :])\
                        .rearrange("p (s h c) -> p s h c", s=2, c=4)
                    for c in range(4):
                        for s in range(2):
                            is_k = j < 2 and s == 1
                            ins = dve.tensor_scalar(dst[:, s, :, 3 - c if is_k else c], src[:, s, :, c],
                                                    -1.0 if c == (3 if is_k else 1) else 1.0, None, ALU.mult)
                ins.then_inc(wT_read, 1)
            dve.wait_ge(wts_in, 16 * len(loads))
            dve.tensor_copy(bv_cols[:, :], spread(bv_col[:, :], 1, P)).then_inc(bv_spread, 1)
            dve.wait_ge(wT_full, 6)
            dve.tensor_tensor(bo_bc[:, :], W1[:, 0:P], bo_bc[:, :], ALU.add).then_inc(wT_read, 1)
            dve.wait_ge(wT_read, 6)

            def copy_xT(c):
                dve.wait_ge(xT_full, c + 1)
                dve.wait_ge(proj_full, NT * c)
                dve.tensor_copy(xT[:, 1:T + 1], W0[:, :]).then_inc(xT_read, 1)

            def lines_a(c):
                dve.wait_ge(proj_read, NT * (c + 1))
                for dst, many, one in products(prodA, 1, 0):
                    ins = dve.tensor_tensor(dst, many, one, ALU.mult)
                chain(ins)
                dve.wait_ge(prodB_done, NPROD * (c + 1))
                chain(dve.tensor_tensor(prodA[:, :, :], prodA[:, :, :], prodB[:, :, :], ALU.subtract))
                ins = dve.tensor_tensor(prodB[:, :, :], prodA[:, :, :], prodA[:, :, :], ALU.mult)
                chain(ins)
                chain(dve.tensor_reduce(nrm[:, :], prodB[:, :, :], AX.X, ALU.add))

            def lines_b(c):
                chain(dve.tensor_scalar(nrm[:, :], nrm[:, :], 1e-24, None, ALU.max))
                dve.tensor_scalar(nhalf[:, :], nrm[:, :], -0.5, None, ALU.mult)
                chain(dve.tensor_scalar(rs_b[:, :].bitcast(I32), nrm[:, :].bitcast(I32), 1, None,
                                        ALU.logical_shift_right))
                chain(dve.tensor_scalar(rs_a[:, :].bitcast(I32), rs_b[:, :].bitcast(I32), -1.0, float(0x5f3759df),
                                        ALU.mult, ALU.add))
                for _ in range(3):
                    chain(dve.tensor_tensor(rs_b[:, :], rs_a[:, :], rs_a[:, :], ALU.mult))
                    chain(dve.tensor_tensor(rs_b[:, :], rs_b[:, :], nhalf[:, :], ALU.mult))
                    chain(dve.scalar_tensor_tensor(out=rs_a[:, :], in0=rs_b[:, :], scalar=1.5, in1=rs_a[:, :],
                                                   op0=ALU.add, op1=ALU.mult))

            def lines_c(c):
                rs = spread(rs_a[:, :].rearrange("p (h o) -> p h o", o=1), 2, LINE)
                chain(dve.scalar_tensor_tensor(out=prodB[:, :, :], in0=prodA[:, :, :], scalar=SPLIT_UP, in1=rs,
                                               op0=ALU.mult, op1=ALU.mult))
                dve.wait_ge(featT_full, HP * c)
                chain(dve.tensor_copy(feat[:, :, 0:LINE], prodB[:, :, :]))
                dve.tensor_tensor(feat[:, :, LINE:2 * LINE], prodB[:, :, :], feat[:, :, 0:LINE], ALU.subtract)\
                    .then_inc(prodB_read, 1)
                dve.wait_ge(prodB_read, c + 1)
                f = feat[:, :, :].rearrange("p (s h) l -> p s h l", s=2)
                dve.tensor_copy(f[:, 0, :, 2 * LINE:4 * LINE], f[:, 0, :, 0:2 * LINE])
                dve.tensor_copy(f[:, 1, :, 2 * LINE:3 * LINE], f[:, 1, :, LINE:2 * LINE])
                dve.tensor_copy(f[:, 1, :, 3 * LINE:4 * LINE], f[:, 1, :, 0:LINE]).then_inc(feat_done, 1)

            def copy_feat(c, par, g):
                dve.wait_ge(featT_full, HP * c + g + 1)
                dve.tensor_copy(qkT[:, par, g, :, :].rearrange("p s n -> p (s n)"),
                                W[(g + 1) % 2][:, :].bitcast(FP16)).then_inc(featT_read, 1)

            def normalise(c, t):
                dve.wait_ge(outT_full, NT * c + t + 1)
                if t == 0:
                    dve.wait_ge(oT_full, c)
                w = W[(t + 1) % 2][:, :].rearrange("p (h n) -> p h n", n=32)
                chain(dve.reciprocal(rden[:, t, :].rearrange("p (h o) -> p h o", o=1), w[:, :, DH:DH + 1]))
                dve.tensor_tensor(o_tok[:, t, :].rearrange("p (h d) -> p h d", d=DH), w[:, :, 0:DH],
                                  spread(rden[:, t, :].rearrange("p (h o) -> p h o", o=1), 2, DH), ALU.mult)\
                    .then_inc(outT_read, 1)

            def residual(c, par):
                dve.wait_ge(y_full, c + 1)
                dve.wait_ge(xres_done, c + 1)
                dve.tensor_tensor(ysum[:, :, :], W0[:, :].rearrange("p (t n) -> p t n", t=NT), xres[:, par, :, :],
                                  ALU.add).then_inc(y_read, 1)
                dve.wait_ge(y_read, c + 1)
                for t in range(NT):
                    ins = dve.bn_stats(stats[:, t, :], ysum[:, t, :])
                chain(ins)
                dve.sem_inc(parted, 1)
                for t in range(NT):
                    ins = dve.bn_aggr(meanvar[:, t, :], stats[:, t, :])
                chain(ins)
                dve.tensor_scalar(vareps[:, :], meanvar[:, :, 1], EPS, None, ALU.add).then_inc(var_done, 1)

            def norm_out(c, par):
                dve.wait_ge(rstd_done, c + 1)
                dve.wait_ge(x1_out[par], 16 * ((c - par) // 2) + 16)
                for t in range(NT):
                    ins = dve.tensor_scalar(x1[:, par, t, :], ysum[:, t, :], meanvar[:, t, 0:1], rstd[:, t:t + 1],
                                            ALU.subtract, ALU.mult)
                ins.then_inc(x1_done, 1)

            def add_bias(c, par):
                dve.wait_ge(xT_full, c + 1)
                dve.tensor_tensor(xres[:, par, :, :], x_in[:, par, :, :],
                                  spread(bo_bc[:, :].rearrange("p (o n) -> p o n", o=1), 1, NT), ALU.add)\
                    .then_inc(xres_done, 1)

            copy_xT(0)
            lines_a(0)
            lines_b(0)
            lines_c(0)
            for g in range(HP):
                copy_feat(0, 0, g)
            add_bias(0, 0)

            def body(b, par, first, last):
                count[0] = 0
                if not last:
                    copy_xT(b + 1)
                if not first:
                    for t in range(NT):
                        normalise(b - 1, t)
                if not last:
                    lines_a(b + 1)
                    lines_b(b + 1)
                    lines_c(b + 1)
                if not first:
                    residual(b - 1, 1 - par)
                if not last:
                    for g in range(HP):
                        copy_feat(b + 1, 1 - par, g)
                if not first:
                    norm_out(b - 1, 1 - par)
                if not last:
                    add_bias(b + 1, 1 - par)
                base[0] = base[0] + count[0]
            per = 4 + 4 + 12 + 2 + 2
            base[0] = count[0]
            body(0, 0, True, False)
            start = base[0]
            with dve.Fori(0, NB // 2 - 1) as i:
                base[0] = start + i * (2 * per)
                body(2 * i + 1, 1, False, False)
                assert count[0] == per
                body(2 * i + 2, 0, False, False)
                assert count[0] == per
            base[0] = start + (NB // 2 - 1) * 2 * per
            body(NB - 1, 1, False, True)
            count[0] = 0
            for t in range(NT):
                normalise(NB - 1, t)
            residual(NB - 1, 1)
            norm_out(NB - 1, 1)


        block_scope.close()
        phase1.close()

        NX = NE + 1
        ctx2 = ctx.enter_context(ExitStack())

        def sb2(name, shape, dt=FP32):
            return ctx2.enter_context(nc.sbuf_tensor(name, shape, dt))

        w_raw = sb2("w_raw", [P, NX, 6, P])
        w_T = sb2("w_T", [P, NX, 6, P])
        wr_raw = sb2("wr_raw", [NE, P])
        wr_T = sb2("wr_T", [P, NE])
        rb_bc = sb2("rb_bc", [P, NE])
        iota_e = sb2("iota_e", [P, NT, NE])
        x1_in = sb2("x1_in", [P, 2, NT, P])
        x1T = sb2("x1T", [P, T])
        rt = {n: sb2("rt_" + n, [P, NT, NE]) for n in ("logit", "prob", "eq", "cand", "one1", "rest", "one2", "cw")}
        rmax = sb2("rmax", [P, NT])
        rmin = sb2("rmin", [P, NT])
        th = sb2("th", [P, 2, T])
        gated = sb2("gated", [P, 2, T])
        hid = sb2("hid", [P, 2, 2, T])
        acc = sb2("acc", [P, NT, P])
        stats2 = sb2("stats2", [P, NT, 6])
        meanvar2 = sb2("meanvar2", [P, NT, 2])
        vareps2 = sb2("vareps2", [P, NT])
        rstd2 = sb2("rstd2", [P, NT])
        res = sb2("res", [P, 2, NT, P])

        w2_in = sem("w2_in"); w2T_full = sem("w2T_full"); w2T_read = sem("w2T_read"); iota_done = sem("iota_done")
        x1_in_done = [sem("x1_in0"), sem("x1_in1")]
        x1T_full = sem("x1T_full"); x1T_read = sem("x1T_read"); logit_full = sem("logit_full")
        logit_read = sem("logit_read"); logit_ready = sem("logit_ready"); tanh_done = sem("tanh_done")
        gu_full = sem("gu_full"); gate_tanh = sem("gate_tanh"); hid_done = sem("hid_done")
        down_full = sem("down_full"); down_read = sem("down_read")
        var2_done = sem("var2_done"); rstd2_done = sem("rstd2_done"); res_done = sem("res_done")
        res_out = [sem("res_out0"), sem("res_out1")]
        step2 = sem("step2")
        wg_v = [Wg_s.rearrange("(a p) d -> p a d", p=P), Wg.rearrange("e (a p) d -> p e a d", p=P)]
        wu_v = [Wu_s.rearrange("(a p) d -> p a d", p=P), Wu.rearrange("e (a p) d -> p e a d", p=P)]
        wd_v = [Wd_s.rearrange("p (a d) -> p a d", d=P), Wd.rearrange("e p (a d) -> p e a d", d=P)]
        loads2 = [(wr_raw[:, :], Wr), (rb_bc[:, :], rb.partition_broadcast(P))]
        for k, v in enumerate((wg_v, wu_v, wd_v)):
            loads2.append((w_raw[:, 0, 2 * k:2 * k + 2, :], v[0]))
            for e in range(NE):
                loads2.append((w_raw[:, 1 + e, 2 * k:2 * k + 2, :], v[1][:, e]))

        def over_pairs(eng, body):
            body(0, 0, 0)
            body(1, 1, 0)
            with eng.Fori(1, NB // 2) as i:
                body(2 * i, 0, i)
                body(2 * i + 1, 1, i)

        block2 = ctx.enter_context(nc.Block())

        @block2.sync
        def _(sp):
            for dst, src in loads2:
                sp.dma_start(dst, src).then_inc(w2_in, 16)

            def load(b, par):
                sp.dma_start(x1_in[:, par], x1_dram[bass.ds(b, 1)].rearrange("a (t p) d -> p (a t) d", p=P))\
                    .then_inc(x1_in_done[par], 16)
            load(0, 0)
            load(1, 1)

            def body(b, par, last):
                sp.wait_ge(res_done, b + 1)
                sp.dma_start(out[bass.ds(b, 1)].rearrange("a (t p) d -> p (a t) d", p=P), res[:, par])\
                    .then_inc(res_out[par], 16)
                if not last:
                    load(b + 2, par)
            with sp.Fori(0, NB // 2 - 1) as i:
                body(2 * i, 0, False)
                body(2 * i + 1, 1, False)
            body(NB - 2, 0, True)
            body(NB - 1, 1, True)
            for par in range(2):
                sp.wait_ge(res_out[par], 16 * NB // 2)

        @block2.gpsimd
        def _(pool):
            pool.iota(iota_e[:, :, :].bitcast(I32), pattern=[[0, NT], [1, NE]], base=-100, channel_multiplier=0)\
                .then_inc(step2, 1)
            pool.wait_ge(step2, 1)
            pool.tensor_copy(iota_e[:, :, :], iota_e[:, :, :].bitcast(I32)).then_inc(iota_done, 1)

            def body(b, par, i):
                pool.wait_ge(var2_done, b + 1)
                pool.tensor_tensor(rstd2[:, :], vareps2[:, :], minus_half[:, :], ALU.pow).then_inc(rstd2_done, 1)
            over_pairs(pool, body)

        @block2.tensor
        def _(pe):
            pe.wait_ge(w2_in, 16 * len(loads2))
            pe.transpose(O[0][:, 0:NE], wr_raw[:, :], ident[0:NE, 0:NE]).then_inc(w2T_full, 1)
            for e in range(NX):
                for h, (a, n) in enumerate(((0, 4), (4, 2))):
                    pe.wait_ge(w2T_read, 2 * e + h) if 2 * e + h > 0 else None
                    for k in range(n):
                        mm = pe.transpose(W[h][:, k * P:(k + 1) * P], w_raw[:, e, a + k, :], ident[:, :])
                    mm.then_inc(w2T_full, 1)
            pe.wait_ge(w2T_read, 2 * NX + 1)

            def down(n, e):
                pe.wait_ge(hid_done, 2 * n + 2)
                pe.wait_ge(down_read, n)
                for t in range(NT):
                    for i in range(2):
                        mm = pe.matmul(O[0][:, t * P:(t + 1) * P], hid[:, e % 2, i, t * P:(t + 1) * P],
                                       w_T[:, e, 4 + i, :], start=(i == 0), stop=(i == 1))
                mm.then_inc(down_full, 1)

            def body(b, par, i):
                pe.wait_ge(x1_in_done[par], 16 * (i + 1))
                for t in range(NT):
                    mm = pe.transpose(W0[:, t * P:(t + 1) * P], x1_in[:, par, t, :], ident[:, :])
                mm.then_inc(x1T_full, 1)
                pe.wait_ge(x1T_read, b + 1)
                for t in range(NT):
                    mm = pe.matmul(W1[:, t * NE:(t + 1) * NE], x1T[:, t * P:(t + 1) * P], wr_T[:, :],
                                   start=True, stop=True)
                mm.then_inc(logit_full, 1)
                for e in range(NX):
                    for h in range(2):
                        n = NX * b + e
                        k = 2 * n + h
                        pe.wait_ge(hid_done, k - 1) if e or h else pe.wait_ge(hid_done, 2 * NX * b)
                        for kk in range(2):
                            mm = pe.matmul(S[h][:, kk * T:(kk + 1) * T], w_T[:, e, 2 * kk + h, :], x1T[:, :],
                                           start=True, stop=True)
                        mm.then_inc(gu_full, 1)
                    if e:
                        down(NX * b + e - 1, e - 1)
                down(NX * b + NX - 1, NX - 1)
            over_pairs(pe, body)

        @block2.scalar
        def _(act):
            def body(b, par, i):
                act.wait_ge(x1T_full, b + 1)
                act.copy(x1T[:, :], W0[:, :]).then_inc(x1T_read, 1)
                act.wait_ge(logit_ready, b + 1)
                act.activation(rt["prob"][:, :, :], rt["logit"][:, :, :], ACT.Tanh, scale=0.5).then_inc(tanh_done, 1)
                for e in range(NX):
                    for h in range(2):
                        act.wait_ge(gu_full, 2 * NX * b + 2 * e + h + 1)
                        if e:
                            act.wait_ge(hid_done, 2 * NX * b + 2 * e + h - 1)
                        act.activation(th[:, h, :], S[h][:, 0:T], ACT.Tanh, scale=0.5).then_inc(gate_tanh, 1)
            over_pairs(act, body)

        @block2.vector
        def _(dve):
            count = [0]
            PER = 14 + 2 * NX + 2

            dve.wait_ge(w2T_full, 1)
            dve.tensor_copy(wr_T[:, :], O[0][:, 0:NE]).then_inc(w2T_read, 1)
            for e in range(NX):
                for h, (a, n) in enumerate(((0, 4), (4, 2))):
                    dve.wait_ge(w2T_full, 2 * e + h + 2)
                    dve.tensor_copy(w_T[:, e, a:a + n, :].rearrange("p k n -> p (k n)"), W[h][:, 0:n * P])\
                        .then_inc(w2T_read, 1)
            dve.wait_ge(iota_done, 1)
            dve.wait_ge(w2_in, 16 * len(loads2))

            def body(b, par, i):
                count[0] = 0

                def chain(ins):
                    ins.then_inc(step2, 1)
                    count[0] += 1
                    dve.wait_ge(step2, PER * b + count[0] + 1)
                L, PR, EQ, CA, O1, RE, O2, CW = (rt[n][:, :, :] for n in
                                                 ("logit", "prob", "eq", "cand", "one1", "rest", "one2", "cw"))

                def bc(v):
                    return spread(v.rearrange("p (t o) -> p t o", o=1), 2, NE)
                dve.wait_ge(logit_full, b + 1)
                dve.tensor_tensor(L, W1[:, 0:NT * NE].rearrange("p (t e) -> p t e", e=NE),
                                  spread(rb_bc[:, :].rearrange("p (o e) -> p o e", o=1), 1, NT), ALU.add)\
                    .then_inc(logit_ready, 1)
                dve.wait_ge(tanh_done, b + 1)
                chain(dve.tensor_scalar(PR, PR, 0.5, 0.5, ALU.mult, ALU.add))

                def first_largest(src, one):
                    chain(dve.tensor_reduce(rmax[:, :], src, AX.X, ALU.max))
                    chain(dve.tensor_tensor(EQ, src, bc(rmax[:, :]), ALU.is_equal))
                    chain(dve.tensor_tensor(CA, EQ, iota_e[:, :, :], ALU.mult))
                    chain(dve.tensor_reduce(rmin[:, :], CA, AX.X, ALU.min))
                    chain(dve.tensor_tensor(one, CA, bc(rmin[:, :]), ALU.is_equal))
                first_largest(PR, O1)
                chain(dve.scalar_tensor_tensor(out=RE, in0=O1, scalar=-4.0, in1=PR, op0=ALU.mult, op1=ALU.add))
                first_largest(RE, O2)
                chain(dve.tensor_tensor(CW, O1, O2, ALU.add))
                chain(dve.tensor_tensor(CW, CW, PR, ALU.mult))
                for e in range(NX + 1):
                    if e < NX:
                        for h in range(2):
                            dve.wait_ge(gate_tanh, 2 * NX * b + 2 * e + h + 1)
                            chain(dve.scalar_tensor_tensor(out=gated[:, h, :], in0=th[:, h, :], scalar=1.0,
                                                           in1=S[h][:, 0:T], op0=ALU.add, op1=ALU.mult))
                            dve.scalar_tensor_tensor(out=hid[:, e % 2, h, :], in0=gated[:, h, :], scalar=0.5,
                                                     in1=S[h][:, T:2 * T], op0=ALU.mult, op1=ALU.mult)\
                                .then_inc(hid_done, 1)
                    if e:
                        dve.wait_ge(down_full, NX * b + e)
                        src = O[0][:, :].rearrange("p (t n) -> p t n", t=NT)
                        if e == 1:
                            dve.tensor_tensor(acc[:, :, :], src, x1_in[:, par, :, :], ALU.add).then_inc(down_read, 1)
                        else:
                            for t in range(NT):
                                ins = dve.scalar_tensor_tensor(out=acc[:, t, :], in0=src[:, t, :],
                                                               scalar=CW[:, t, e - 2:e - 1], in1=acc[:, t, :],
                                                               op0=ALU.mult, op1=ALU.add)
                            ins.then_inc(down_read, 1)
                        dve.wait_ge(down_read, NX * b + e)
                for t in range(NT):
                    ins = dve.bn_stats(stats2[:, t, :], acc[:, t, :])
                chain(ins)
                dve.sem_inc(parted, 1)
                for t in range(NT):
                    ins = dve.bn_aggr(meanvar2[:, t, :], stats2[:, t, :])
                chain(ins)
                dve.tensor_scalar(vareps2[:, :], meanvar2[:, :, 1], EPS, None, ALU.add).then_inc(var2_done, 1)
                dve.wait_ge(rstd2_done, b + 1)
                dve.wait_ge(res_out[par], 16 * i)
                for t in range(NT):
                    ins = dve.tensor_scalar(res[:, par, t, :], acc[:, t, :], meanvar2[:, t, 0:1], rstd2[:, t:t + 1],
                                            ALU.subtract, ALU.mult)
                ins.then_inc(res_done, 1)
                assert count[0] == PER, count[0]
            over_pairs(dve, body)


_INS = ["L0_attn_x", "L0_attn_W1_q", "L0_attn_W2_q", "L0_attn_W1_k", "L0_attn_W2_k", "L0_attn_Wv", "L0_attn_bv",
        "L0_attn_Wo", "L0_attn_bo", "L0_ffn_Wg_s", "L0_ffn_Wu_s", "L0_ffn_Wd_s", "L0_ffn_Wg", "L0_ffn_Wu",
        "L0_ffn_Wd", "L0_ffn_Wr", "L0_ffn_rb"]


def kernel(**inputs):
    import numpy as np
    import concourse.bacc as bacc
    from concourse.bass_utils import run_bass_kernel_spmd

    nc = bacc.Bacc("TRN2", target_bir_lowering=False, num_devices=1)
    arrays, args = {}, []
    for name in _INS:
        a = np.ascontiguousarray(inputs[name])
        arrays[f"in_{name}"] = a
        args.append(nc.dram_tensor(f"in_{name}", a.shape, mybir.dt.from_np(a.dtype), kind="ExternalInput").ap())
    shape = inputs["L0_attn_x"].shape
    out = nc.dram_tensor("out_0", shape, FP32, kind="ExternalOutput").ap()
    block_program(nc, *args, out)
    return run_bass_kernel_spmd(nc, [arrays], core_ids=[0]).results[0]["out_0"]
```

```python
import concourse.bass as bass
from concourse import mybir
from contextlib import ExitStack

FP32 = mybir.dt.float32
FP16 = mybir.dt.float16
I32 = mybir.dt.int32
ALU = mybir.AluOpType
ACT = mybir.ActivationFunctionType
AX = mybir.AxisListType

P = 128
T = 512
NT = T // P
H = 16
DH = P // H
HP = H // 4
LINE = 6
FEAT = 32
HH = 2 * H
SPLIT_UP = 1024.0
SCALE = 6.0 ** -0.5
NE = 8
FF = 256
EPS = 1e-5
UP = 64.0
H_UP = 8.0
ROW = P + 2
UNIT = 2 * P

CHUNK = 1024
NCHUNK = 5
PIECES = {
    (0, 0): (0, 0), (0, 3): (0, 512), (0, 1): (0, 640),
    (1, 0): (1, 0), (1, 3): (1, 512), (1, 1): (1, 640),
    (0, 2): (2, 0), (2, 0): (2, 512), (1, 2): (2, 256),
    (2, 3): (3, 0), (2, 1): (3, 128), (3, 0): (3, 512),
    (2, 2): (4, 512), (3, 3): (4, 0), (3, 1): (4, 128), (3, 2): (4, 768),
}
BANK_MATE = {(1, 2): (0, 2), (3, 2): (2, 2)}
SQUARES = {
    0: [(0, 1, 128), (512, 2, 128)],
    1: [(0, 1, 128), (512, 2, 128)],
    2: [(0, 3, 256)],
    3: [(0, 2, 128), (512, 1, 128)],
    4: [(0, 2, 128), (512, 2, 256)],
}


def spread(ap, dim, n):
    shape = list(ap.shape)
    shape[dim] = n
    return ap.broadcast_to(shape)


def block_program(nc, x, W1_q, W2_q, W1_k, W2_k, Wv, bv, Wo, bo, Wg_s, Wu_s, Wd_s, Wg, Wu, Wd, Wr, rb, out):
    NB = x.shape[0]
    ctx = ExitStack()
    with ctx:
        def sb(name, shape, dt=FP32):
            return ctx.enter_context(nc.sbuf_tensor(name, shape, dt))

        def pb(name, shape, dt=FP32):
            return ctx.enter_context(nc.psum_tensor(name, shape, dt))

        def sem(name):
            return ctx.enter_context(nc.semaphore(name))

        phase1 = ExitStack()

        def sb1(name, shape, dt=FP32):
            return phase1.enter_context(nc.sbuf_tensor(name, shape, dt))

        ident = sb("ident", [P, P])
        ident16 = sb("ident16", [P, P], FP16)
        next_slot = sb("next_slot", [P, NE])
        pad_rows = sb("pad_rows", [P, 2, ROW])
        minus_half = sb("minus_half", [P, 4])
        w_nat = sb1("w_nat", [P, 8, P])
        w_allT = sb1("w_allT", [P, 3 * P])
        w_prevT = sb1("w_prevT", [P, P])
        w_oT = sb1("w_oT", [P, P])
        bv_col = sb1("bv_col", [P, 1])
        bv_cols = sb1("bv_cols", [P, P])
        bo_bc = sb1("bo_bc", [P, P])
        x_in = sb1("x_in", [P, 2, NT, P])
        xres = sb1("xres", [P, 2, NT, P])
        xT = sb1("xT", [P, T + 1])
        p12 = sb1("p12", [P, 2, 2, NT, H, 4])
        v_aug = sb1("v_aug", [P, 2, NT, H, 32])
        prodA = sb1("prodA", [P, NT * HH, LINE])
        prodB = sb1("prodB", [P, NT * HH, LINE])
        nrm = sb1("nrm", [P, NT * HH])
        nhalf = sb1("nhalf", [P, NT * HH])
        rs_a = sb1("rs_a", [P, NT * HH])
        rs_b = sb1("rs_b", [P, NT * HH])
        feat = sb1("feat", [P, NT * HH, FEAT], FP16)
        qkT = sb1("qkT", [P, 2, HP, 2, T], FP16)
        probs = sb1("probs", [P, 2, NCHUNK, CHUNK])
        oT_raw = sb1("oT_raw", [P, HP, T])
        rden = sb1("rden", [P, NT, H])
        o_tok = sb1("o_tok", [P, NT, P])
        oT = sb1("oT", [P, T])
        ysum = sb1("ysum", [P, NT, P])
        stats = sb1("stats", [P, NT, 6])
        meanvar = sb1("meanvar", [P, NT, 2])
        vareps = sb1("vareps", [P, NT])
        rstd = sb1("rstd", [P, NT])
        x1 = sb1("x1", [P, 2, NT, P])
        xrow = sb1("xrow", [P, 2, NT, 2, ROW])
        x1T = sb1("x1T", [P, 2, 2, T], FP16)
        wr_raw = sb1("wr_raw", [NE, P])
        wr_T = sb1("wr_T", [P, 2, NE], FP16)
        rb_bc = sb1("rb_bc", [P, NE])
        rb4 = sb1("rb4", [P, NT, NE])
        iota_i = sb1("iota_i", [P, NT, NE], I32)
        iota_e = sb1("iota_e", [P, NT, NE])
        tri = sb1("tri", [P, P], FP16)
        ones16 = sb1("ones16", [P, P], FP16)
        picks = sb1("picks", [P, NT, NE], FP16)
        rt = {n: sb1("rt_" + n, [P, NT, NE]) for n in ("logit", "prob", "eq", "cand", "rest", "slot")}
        one = sb1("one", [P, 2, NT, NE])
        oneslot = sb1("oneslot", [P, 2, NT, NE])
        rmax = sb1("rmax", [P, 2, NT])
        rmin = sb1("rmin", [P, NT])
        slot_f = sb1("slot_f", [P, 2, NT])
        slot_i = sb1("slot_i", [P, 2, 2, NT], I32)
        place_i = sb1("place_i", [P, 2, NT], I32)
        NTOK = NB * T
        CAP = NTOK + UNIT
        TAIL = NE * CAP
        x1_dram = nc.dram_tensor("x1_scratch", (NB, T, P), FP32).ap()
        x1T_dram = nc.dram_tensor("x1T_scratch", (NB, P, 2, T), FP16).ap()
        rows_dram = nc.dram_tensor("rows_scratch", (TAIL + UNIT, ROW), FP32).ap()
        z_dram = nc.dram_tensor("z_scratch", (2 * NTOK, P), FP32).ap()

        S = [pb(f"S{i}", [P, CHUNK]) for i in range(2)]
        O = [pb(f"O{i}", [P, T]) for i in range(2)]
        W0 = pb("W0", [P, T])
        W1 = pb("W1", [P, T])
        W = [W0, W1]

        wts_in = sem("wts_in"); consts = sem("consts"); xin_in = [sem("xin_in0"), sem("xin_in1")]
        wT_full = sem("wT_full"); wT_read = sem("wT_read")
        xT_full = sem("xT_full"); xT_read = sem("xT_read")
        proj_full = sem("proj_full"); proj_read = sem("proj_read")
        prodB_done = sem("prodB_done"); prodB_read = sem("prodB_read")
        feat_done = sem("feat_done"); featT_full = sem("featT_full"); featT_read = sem("featT_read")
        s_full = sem("s_full"); s_exp = sem("s_exp"); masked = sem("masked"); pv_done = sem("pv_done")
        o_read = sem("o_read")
        outT_full = sem("outT_full"); outT_read = sem("outT_read")
        oT_full = sem("oT_full"); oT_read = sem("oT_read")
        y_full = sem("y_full"); y_read = sem("y_read")
        var_done = sem("var_done"); rstd_done = sem("rstd_done")
        x1_done = sem("x1_done"); x1_out = [sem("x1_out0"), sem("x1_out1")]
        dve_step = sem("dve_step"); pool_step = sem("pool_step")
        xres_done = sem("xres_done"); parted = sem("parted"); pad_done = sem("pad_done"); split_done = sem("split_done")
        x1T_full = sem("x1T_full"); x1T_read = sem("x1T_read"); x1T_out = [sem("x1T_out0"), sem("x1T_out1")]
        logit_full = sem("logit_full"); logit_read = sem("logit_read"); tanh_done = sem("tanh_done")
        picks_done = sem("picks_done"); rank_full = sem("rank_full"); rank_read = sem("rank_read")
        rows_ready = sem("rows_ready"); rows_out = [sem("rows_out0"), sem("rows_out1")]; mate_done = sem("mate_done"); bv_spread = sem("bv_spread")

        loads = [
            (w_nat[0:64, 0, :], W1_q[:, 0:P]), (w_nat[64:128, 0, :], W1_k),
            (w_nat[0:64, 1, :], W2_q[:, 0:P]), (w_nat[64:128, 1, :], W2_k),
            (w_nat[:, 2, :], Wv), (w_nat[0:64, 3, :], W1_q[:, P:2 * P]), (w_nat[64:128, 3, :], W2_q[:, P:2 * P]),
            (w_nat[:, 4, :], Wo),
            (bv_col[:, :], bv.rearrange("(p o) -> p o", o=1)),
            (bo_bc[:, :], bo.partition_broadcast(P)), (wr_raw[:, :], Wr), (rb_bc[:, :], rb.partition_broadcast(P)),
        ]

        CONSTS = 11 + NE

        def over_batches(eng, body):
            body(0, 0, True, False)
            body(1, 1, False, False)
            with eng.Fori(1, NB // 2 - 1) as i:
                body(2 * i, 0, False, False)
                body(2 * i + 1, 1, False, False)
            body(NB - 2, 0, False, False)
            body(NB - 1, 1, False, True)

        def routes(b):
            return not (isinstance(b, int) and b < 2)

        def products(dst, many, one):
            d = dst[:, :, :].rearrange("p (s h) l -> p s h l", s=2)
            q_many, k_many = (p12[:, many, s].rearrange("p t h c -> p (t h) c") for s in range(2))
            q_one, k_one = (p12[:, one, s].rearrange("p t h c -> p (t h) c") for s in range(2))
            for i, l0, n in ((0, 0, 3), (1, 3, 2), (2, 5, 1)):
                yield d[:, 0, :, l0:l0 + n], q_many[:, :, i + 1:4], spread(q_one[:, :, i:i + 1], 2, n)
            for j, l0, n in ((1, 0, 1), (2, 1, 2), (3, 3, 3)):
                yield d[:, 1, :, l0:l0 + n], spread(k_many[:, :, j:j + 1], 2, n), k_one[:, :, 0:n]

        block_scope = ExitStack()
        block = block_scope.enter_context(nc.Block())

        @block.sync
        def _(sp):
            for dst, src in loads:
                sp.dma_start(dst, src).then_inc(wts_in, 16)
            for par in range(2):
                sp.sem_inc(x1_out[par], 16)
                sp.sem_inc(x1T_out[par], 16)

            def body(b, par, first, last):
                if not first:
                    sp.wait_ge(x1_done, b)
                    sp.dma_start(x1_dram[bass.ds(b - 1, 1)].rearrange("a (t p) d -> p (a t) d", p=P), x1[:, 1 - par])\
                        .then_inc(x1_out[1 - par], 16)
                if routes(b):
                    store_x1T(b - 2, par)

            def store_x1T(c, par):
                sp.wait_ge(x1T_read, c + 1)
                sp.dma_start(x1T_dram[bass.ds(c, 1)].rearrange("a p s n -> p (a s) n"), x1T[:, par])\
                    .then_inc(x1T_out[par], 16)
            over_batches(sp, body)
            store_x1T(NB - 2, 0)
            store_x1T(NB - 1, 1)
            for par in range(2):
                sp.wait_ge(x1T_out[par], 16 * NB // 2 + 16)
            sp.wait_ge(x1_done, NB)
            sp.dma_start(x1_dram[NB - 1].rearrange("(t p) d -> p t d", p=P), x1[:, 1]).then_inc(x1_out[1], 16)
            for par in range(2):
                sp.wait_ge(x1_out[par], 16 * NB // 2 + 16)

        @block.gpsimd
        def _(pool):
            steps = [0]

            def then_wait(ins):
                steps[0] += 1
                ins.then_inc(pool_step, 1)
                pool.wait_ge(pool_step, steps[0])
            pool.memset(ident[:, :], 0.0).then_inc(pool_step, 1)
            pool.memset(ident16[:, :], 0.0).then_inc(pool_step, 1)
            pool.wait_ge(pool_step, 2)
            for m in (ident, ident16):
                pool.affine_select(out=m[:, :], in_=m[:, :], compare_op=ALU.not_equal, fill=1.0, base=0,
                                   pattern=[[-1, P]], channel_multiplier=1).then_inc(consts, 1)
            pool.memset(minus_half[:, :], -0.5).then_inc(consts, 1)
            pool.memset(xT[:, 0:1], 0.0).then_inc(consts, 1)
            pool.memset(feat[:, :, :], 0.0).then_inc(consts, 1)
            pool.memset(v_aug[:, :, :, :, :], 0.0).then_inc(pool_step, 1)
            pool.wait_ge(pool_step, 3)
            for par in range(2):
                pool.memset(v_aug[:, par, :, :, DH:DH + 1].rearrange("p t h o -> p (t h) o"), 1.0)\
                    .then_inc(consts, 1)
            pool.iota(iota_i[:, :, :], pattern=[[0, NT], [1, NE]], base=-100, channel_multiplier=0)\
                .then_inc(consts, 1)
            pool.iota(place_i[:, :, :], pattern=[[NTOK, 2], [P, NT]], base=0, channel_multiplier=1).then_inc(consts, 1)
            pool.memset(ones16[:, :], 1.0).then_inc(consts, 1)
            pool.wait_ge(consts, 10)
            pool.affine_select(out=tri[:, :], in_=ones16[:, :], compare_op=ALU.is_gt, fill=0.0, base=0,
                               pattern=[[1, P]], channel_multiplier=-1).then_inc(consts, 1)
            for e in range(NE):
                pool.memset(next_slot[:, e:e + 1], float(e * CAP)).then_inc(consts, 1)
            pool.memset(pad_rows[:, :, 0:P + 1], 0.0).then_inc(pad_done, 1)
            pool.memset(pad_rows[:, :, P + 1:P + 2].bitcast(I32), 2 * NTOK).then_inc(pad_done, 1)
            pool.wait_ge(pad_done, 2)
            for par in range(2):
                pool.dma_start(rows_dram[TAIL + par * P:TAIL + (par + 1) * P], pad_rows[:, par, :])\
                    .then_inc(rows_out[par], 16)

            def dispatch(c, par):
                pool.wait_ge(rows_ready, c + 1)
                pool.sem_inc(parted, 1)
                for t in range(NT):
                    for k in range(2):
                        pool.indirect_dma_start(
                            out=rows_dram, in_=xrow[:, par, t, k, :], in_offset=None,
                            out_offset=bass.IndirectOffsetOnAxis(ap=slot_i[:, par, k, t:t + 1], axis=0),
                            bounds_check=TAIL - 1, oob_is_err=False).then_inc(rows_out[par], 16)

            def line_products(c):
                pool.wait_ge(proj_read, NT * (c + 1))
                pool.wait_ge(prodB_read, c)
                for dst, many, one in products(prodB, 0, 1):
                    pool.tensor_tensor(dst, many, one, ALU.mult).then_inc(prodB_done, 1)

            def inv_std(c):
                pool.wait_ge(var_done, c + 1)
                pool.tensor_tensor(rstd[:, :], vareps[:, :], minus_half[:, :], ALU.pow).then_inc(rstd_done, 1)

            def mask(b, g):
                for c in range(NCHUNK):
                    pool.wait_ge(s_exp, NCHUNK * HP * b + NCHUNK * g + c + 1)
                    pool.sem_inc(parted, 1)
                    for col, n, step in SQUARES[c]:
                        v = probs[:, g % 2, c, col:col + (n - 1) * step + P] if step == P or n == 1 else None
                        if v is None:
                            v = probs[:, g % 2, c, col:col + n * step].rearrange("p (n k) -> p n k", n=n)[:, :, 0:P]
                        else:
                            v = v.rearrange("p (n k) -> p n k", n=n)
                        pool.affine_select(out=v, in_=v, compare_op=ALU.is_ge, fill=0.0, base=0,
                                           pattern=[[0, n], [1, P]], channel_multiplier=-1).then_inc(masked, 1)
            line_products(0)

            def body(b, par, first, last):
                mask(b, 0)
                mask(b, 1)
                if not last:
                    line_products(b + 1)
                mask(b, 2)
                if not first:
                    inv_std(b - 1)
                mask(b, 3)
                if routes(b):
                    dispatch(b - 2, par)
            over_batches(pool, body)
            inv_std(NB - 1)
            dispatch(NB - 2, 0)
            dispatch(NB - 1, 1)
            for par in range(2):
                pool.wait_ge(rows_out[par], 2 * NT * 16 * NB // 2 + 16)
        NMASK = sum(len(v) for v in SQUARES.values())
        NPROD = 6

        @block.tensor
        def _(pe):
            pe.wait_ge(consts, CONSTS)
            pe.wait_ge(wts_in, 16 * len(loads))
            for j in range(5):
                if j >= 2:
                    pe.wait_ge(wT_read, j - 1)
                pe.transpose(W[j % 2][:, 0:P], w_nat[:, j, :], ident[:, :]).then_inc(wT_full, 1)

            def transpose_x(c, par):
                pe.wait_ge(xin_in[par], 16 * (c // 2 + 1) if isinstance(c, int) else 16 * ((c - par) // 2 + 1))
                for t in range(NT):
                    mm = pe.transpose(W0[:, t * P:(t + 1) * P], x_in[:, par, t, :], ident[:, :])
                mm.then_inc(xT_full, 1)

            def project(c, t):
                w = W[(t + 1) % 2]
                if t == 0:
                    pe.wait_ge(xT_read, c + 1)
                if t >= 2:
                    pe.wait_ge(proj_read, NT * c + t - 1)
                pe.matmul(w[:, 0:3 * P], xT[:, 1 + t * P:1 + (t + 1) * P], w_allT[:, :], start=True, stop=False,
                          skip_group_check=True)
                pe.matmul(w[:, 0:2 * P].rearrange("p (a n) -> p a n", a=2)[:, :, 0:H * 4], xT[:, t * P:(t + 1) * P],
                          w_prevT[:, :].rearrange("p (a n) -> p a n", a=2), start=False, stop=True,
                          skip_group_check=True)\
                    .then_inc(proj_full, 1)

            def transpose_feat(c, g):
                w = W[(g + 1) % 2][:, :].bitcast(FP16).rearrange("p (s n) -> p s n", s=2)
                if g == 0:
                    pe.wait_ge(feat_done, c + 1)
                else:
                    pe.wait_ge(featT_read, HP * c + g - 1)
                for s in range(2):
                    for t in range(NT):
                        first = s * NT * H + t * H + 4 * g
                        mm = pe.transpose(w[:, s, t * P:(t + 1) * P],
                                          feat[:, first:first + 4, :].rearrange("p h f -> p (h f)"), ident16[:, :])
                mm.then_inc(featT_full, 1)

            MATES = len(BANK_MATE)
            mates = [0]

            def scores(b, par, g, chunks):
                if chunks[0] == 0:
                    mates[0] = 0
                for c in chunks:
                    n = NCHUNK * HP * b + NCHUNK * g + c
                    if not (isinstance(n, int) and n < 2):
                        pe.wait_ge(s_exp, n - 1)
                    if c == 0:
                        pe.wait_ge(featT_read, HP * b + g + 1)
                    for (j, kb), (cc, col) in PIECES.items():
                        if cc == c:
                            q = qkT[32 * j:32 * j + 32, par, g, 0, kb * P:T]
                            k = qkT[32 * j:32 * j + 32, par, g, 1, kb * P:(kb + 1) * P]
                            if (j, kb) in BANK_MATE:
                                mates[0] += 1
                                pe.wait_ge(mate_done, MATES * (HP * b + g) + mates[0])
                            mm = pe.matmul(S[(g + c) % 2][:, col:col + T - kb * P], k, q, start=True, stop=True)
                            if (j, kb) in BANK_MATE.values():
                                mm.then_inc(mate_done, 1)
                    mm.then_inc(s_full, 1)

            def weigh(b, par, g):
                pe.wait_ge(masked, NMASK * (HP * b + g + 1))
                n = HP * b + g
                if not (isinstance(n, int) and n < 2):
                    pe.wait_ge(o_read, n - 1)
                for kb in range(NT):
                    for j in range(4):
                        c, col = PIECES[(j, kb)]
                        mm = pe.matmul(O[g % 2][32 * j:32 * j + 32, kb * P:T], v_aug[:, par, kb, 4 * g + j, :],
                                       probs[:, g % 2, c, col:col + T - kb * P], start=(kb == 0), stop=(kb == NT - 1),
                                       skip_group_check=True)
                mm.then_inc(pv_done, 1)

            def transpose_out(c, t, after):
                if t == 0:
                    if isinstance(c, int) and c == NB - 1:
                        pe.wait_ge(rank_read, c)
                    pe.wait_ge(o_read, HP * (c + 1))
                    if after:
                        pe.wait_ge(proj_read, NT * (c + 3))
                    else:
                        pe.wait_ge(y_read, c)
                elif t > 1:
                    pe.wait_ge(outT_read, NT * c + t - 1)
                for g in range(HP):
                    mm = pe.transpose(W[(t + 1) % 2][:, g * P:(g + 1) * P], oT_raw[:, g, t * P:(t + 1) * P], ident[:, :])
                mm.then_inc(outT_full, 1)

            def transpose_o(c):
                pe.wait_ge(outT_read, NT * (c + 1))
                for t in range(NT):
                    mm = pe.transpose(W0[:, t * P:(t + 1) * P], o_tok[:, t, :], ident[:, :])
                mm.then_inc(oT_full, 1)

            def project_out(c):
                pe.wait_ge(oT_read, c + 1)
                for t in range(NT):
                    mm = pe.matmul(W0[:, t * P:(t + 1) * P], oT[:, t * P:(t + 1) * P], w_oT[:, :], start=True, stop=True)
                mm.then_inc(y_full, 1)

            pe.wait_ge(wT_read, 5)
            pe.wait_ge(bv_spread, 1)
            pe.matmul(W1[:, 0:P], bv_cols[:, :], w_oT[:, :], start=True, stop=True).then_inc(wT_full, 1)
            pe.transpose(W0[:, 0:NE], wr_raw[:, :], ident[0:NE, 0:NE]).then_inc(wT_full, 1)
            pe.wait_ge(wT_read, 7)
            transpose_x(0, 0)
            for t in range(NT):
                project(0, t)
            pe.wait_ge(proj_read, NT)
            for g in range(HP):
                transpose_feat(0, g)

            def transpose_x1(c, par):
                pe.wait_ge(split_done, c + 1)
                pe.wait_ge(rank_read, c + 1)
                if not (isinstance(c, int) and c == NB - 1):
                    pe.wait_ge(outT_read, NT * (c + 1) + 3)
                halves = xrow[:, par, :, 0, 0:P].bitcast(FP16)
                w = W1[:, :].bitcast(FP16).rearrange("p (s n) -> p s n", s=2)
                for s in range(2):
                    for t in range(NT):
                        mm = pe.transpose(w[:, s, t * P:(t + 1) * P], halves[:, t, s * P:(s + 1) * P], ident16[:, :])
                mm.then_inc(x1T_full, 1)

            def router(c, par):
                pe.wait_ge(x1T_read, c + 1)
                for t in range(NT):
                    for n, (a, w) in enumerate(((0, 0), (0, 1), (1, 0))):
                        mm = pe.matmul(W1[:, t * NE:(t + 1) * NE], x1T[:, par, a, t * P:(t + 1) * P], wr_T[:, w, :],
                                       start=(n == 0), stop=(n == 2))
                mm.then_inc(logit_full, 1)

            def ranks(c):
                pe.wait_ge(picks_done, c + 1)
                pe.matmul(W1[:, 0:NT * NE], tri[:, :], picks[:, :, :].rearrange("p t e -> p (t e)"), start=True,
                          stop=False, skip_group_check=True)
                for t in range(NT):
                    n = NT - t
                    src = spread(picks[:, t:t + 1, :], 1, n)
                    mm = pe.matmul(W1[:, (t + 1) * NE:(NT + 1) * NE].rearrange("p (n e) -> p n e", n=n), ones16[:, :],
                                   src, start=False, stop=(t == NT - 1), skip_group_check=True)
                mm.then_inc(rank_full, 1)

            def body(b, par, first, last):
                scores(b, par, 0, (0, 1))
                if not first:
                    weigh(b - 1, 1 - par, 3)
                pe.wait_ge(featT_read, HP * (b + 1))
                if routes(b):
                    pe.wait_ge(rank_read, b - 1)
                if not last:
                    transpose_x(b + 1, 1 - par)
                scores(b, par, 0, (2, 3, 4))
                if not last:
                    project(b + 1, 0)
                    project(b + 1, 1)
                scores(b, par, 1, (0, 1))
                weigh(b, par, 0)
                scores(b, par, 1, (2, 3, 4))
                if not last:
                    project(b + 1, 2)
                    project(b + 1, 3)
                if not first:
                    for t in range(NT):
                        transpose_out(b - 1, t, not last)
                scores(b, par, 2, (0, 1))
                weigh(b, par, 1)
                scores(b, par, 2, (2, 3, 4))
                if routes(b):
                    transpose_x1(b - 2, par)
                if not first:
                    transpose_o(b - 1)
                scores(b, par, 3, (0, 1))
                weigh(b, par, 2)
                if routes(b):
                    router(b - 2, par)
                if not first:
                    project_out(b - 1)
                scores(b, par, 3, (2, 3, 4))
                if routes(b):
                    pe.wait_ge(logit_read, b - 1)
                if not last:
                    if not first:
                        pe.wait_ge(y_read, b)
                    else:
                        pe.wait_ge(proj_read, 2 * NT)
                    for g in range(HP):
                        transpose_feat(b + 1, g)
                if routes(b):
                    if not last:
                        pe.wait_ge(featT_read, HP * (b + 1) + 3)
                    ranks(b - 2)
            over_batches(pe, body)
            weigh(NB - 1, 1, 3)
            for t in range(NT):
                transpose_out(NB - 1, t, False)
            transpose_o(NB - 1)
            project_out(NB - 1)
            for c in (NB - 2, NB - 1):
                transpose_x1(c, c % 2)
                router(c, c % 2)
                ranks(c)

        @block.scalar
        def _(act):
            def copy_projection(c, par, t):
                act.wait_ge(proj_full, NT * c + t + 1)
                if t == 0:
                    act.wait_ge(prodB_done, NPROD * c)
                    act.wait_ge(prodB_read, c)
                    if not (isinstance(c, int) and c < 2):
                        act.wait_ge(pv_done, HP * (c - 1))
                act.copy(p12[:, :, :, t].rearrange("p a s h c -> p (a s) (h c)"),
                         W[(t + 1) % 2][:, 0:2 * P].rearrange("p (a n) -> p a n", a=4))
                act.copy(v_aug[:, par, t, :, 0:DH], W[(t + 1) % 2][:, 2 * P:3 * P].rearrange("p (h d) -> p h d", d=DH))\
                    .then_inc(proj_read, 1)

            def exps(b, g, chunks):
                for c in chunks:
                    n = HP * b + g
                    act.wait_ge(s_full, NCHUNK * n + c + 1)
                    if c == 0 and not (isinstance(n, int) and n < 2):
                        act.wait_ge(pv_done, n - 1)
                    act.activation(probs[:, g % 2, c, :], S[(g + c) % 2][:, :], ACT.Exp,
                                   scale=-SCALE / SPLIT_UP ** 2).then_inc(s_exp, 1)

            def copy_out(b, g):
                act.wait_ge(pv_done, HP * b + g + 1)
                if g == 0:
                    act.wait_ge(outT_full, NT * b)
                act.copy(oT_raw[:, g, :], O[g % 2][:, :]).then_inc(o_read, 1)

            def copy_oT(c):
                act.wait_ge(oT_full, c + 1)
                act.copy(oT[:, :], W0[:, :]).then_inc(oT_read, 1)

            def copy_x1T(c, par):
                act.wait_ge(x1T_full, c + 1)
                act.wait_ge(x1T_out[par], 16 * ((c - par) // 2) + 16)
                act.copy(x1T[:, par].rearrange("p s n -> p (s n)"), W1[:, :].bitcast(FP16)).then_inc(x1T_read, 1)

            def tanh_logits(c):
                act.wait_ge(logit_read, c + 1)
                act.activation(rt["prob"][:, :, :], rt["logit"][:, :, :], ACT.Tanh, scale=0.5).then_inc(tanh_done, 1)

            def load_x(c, par):
                act.wait_ge(xres_done, c - 1) if not (isinstance(c, int) and c < 2) else None
                act.dma_start(x_in[:, par], x[bass.ds(c, 1)].rearrange("a (t p) d -> p (a t) d", p=P))\
                    .then_inc(xin_in[par], 16)

            load_x(0, 0)
            load_x(1, 1)
            for t in range(NT):
                copy_projection(0, 0, t)

            def body(b, par, first, last):
                if not first and not last:
                    load_x(b + 1, 1 - par)
                exps(b, 0, (0, 1, 2))
                if not first:
                    copy_out(b - 1, 3)
                exps(b, 0, (3, 4))
                if not last:
                    copy_projection(b + 1, 1 - par, 0)
                    copy_projection(b + 1, 1 - par, 1)
                exps(b, 1, (0, 1, 2))
                if first:
                    copy_out(b, 0)
                exps(b, 1, (3, 4))
                if not last:
                    copy_projection(b + 1, 1 - par, 2)
                    copy_projection(b + 1, 1 - par, 3)
                exps(b, 2, (0,))
                if not first:
                    copy_out(b, 0)
                exps(b, 2, (1, 2))
                copy_out(b, 1)
                exps(b, 2, (3, 4))
                if routes(b):
                    copy_x1T(b - 2, par)
                if not first:
                    copy_oT(b - 1)
                exps(b, 3, (0, 1, 2))
                copy_out(b, 2)
                if routes(b):
                    tanh_logits(b - 2)
                exps(b, 3, (3, 4))
            over_batches(act, body)
            copy_out(NB - 1, 3)
            copy_oT(NB - 1)
            for c in (NB - 2, NB - 1):
                copy_x1T(c, c % 2)
                tanh_logits(c)

        @block.vector
        def _(dve):
            base, count = [0], [0]

            def chain(ins):
                ins.then_inc(dve_step, 1)
                count[0] += 1
                dve.wait_ge(dve_step, base[0] + count[0])

            dve.wait_ge(consts, CONSTS)
            for j in range(5):
                dve.wait_ge(wT_full, j + 1)
                src = W[j % 2][:, 0:P]
                if j == 2:
                    ins = dve.tensor_copy(w_allT[:, 2 * P:3 * P], src)
                elif j == 4:
                    ins = dve.tensor_copy(w_oT[:, :], src)
                else:
                    src = src.rearrange("p (s h c) -> p s h c", s=2, c=4)
                    dst = (w_allT[:, j * P:(j + 1) * P] if j < 2 else w_prevT[:, :])\
                        .rearrange("p (s h c) -> p s h c", s=2, c=4)
                    for c in range(4):
                        for s in range(2):
                            is_k = j < 2 and s == 1
                            ins = dve.tensor_scalar(dst[:, s, :, 3 - c if is_k else c], src[:, s, :, c],
                                                    -1.0 if c == (3 if is_k else 1) else 1.0, None, ALU.mult)
                ins.then_inc(wT_read, 1)
            dve.wait_ge(wts_in, 16 * len(loads))
            dve.tensor_copy(bv_cols[:, :], spread(bv_col[:, :], 1, P)).then_inc(bv_spread, 1)
            dve.wait_ge(wT_full, 6)
            dve.tensor_tensor(bo_bc[:, :], W1[:, 0:P], bo_bc[:, :], ALU.add).then_inc(wT_read, 1)
            dve.wait_ge(wT_full, 7)
            dve.tensor_scalar(wr_T[:, 0, :], W0[:, 0:NE], UP, None, ALU.mult).then_inc(rank_read, 1)
            dve.wait_ge(rank_read, 1)
            dve.scalar_tensor_tensor(out=wr_T[:, 1, :], in0=W0[:, 0:NE], scalar=UP, in1=wr_T[:, 0, :], op0=ALU.mult,
                                     op1=ALU.subtract).then_inc(wT_read, 1)
            dve.tensor_copy(iota_e[:, :, :], iota_i[:, :, :])
            dve.tensor_copy(rb4[:, :, :], spread(rb_bc[:, :].rearrange("p (o e) -> p o e", o=1), 1, NT))
            dve.wait_ge(wT_read, 7)

            def copy_xT(c):
                dve.wait_ge(xT_full, c + 1)
                dve.wait_ge(proj_full, NT * c)
                dve.tensor_copy(xT[:, 1:T + 1], W0[:, :]).then_inc(xT_read, 1)

            def lines_a(c):
                dve.wait_ge(proj_read, NT * (c + 1))
                for dst, many, one in products(prodA, 1, 0):
                    ins = dve.tensor_tensor(dst, many, one, ALU.mult)
                chain(ins)
                dve.wait_ge(prodB_done, NPROD * (c + 1))
                chain(dve.tensor_tensor(prodA[:, :, :], prodA[:, :, :], prodB[:, :, :], ALU.subtract))
                ins = dve.tensor_tensor(prodB[:, :, :], prodA[:, :, :], prodA[:, :, :], ALU.mult)
                chain(ins)
                chain(dve.tensor_reduce(nrm[:, :], prodB[:, :, :], AX.X, ALU.add))

            def lines_b(c):
                chain(dve.tensor_scalar(nrm[:, :], nrm[:, :], 1e-24, None, ALU.max))
                dve.tensor_scalar(nhalf[:, :], nrm[:, :], -0.5, None, ALU.mult)
                chain(dve.tensor_scalar(rs_b[:, :].bitcast(I32), nrm[:, :].bitcast(I32), 1, None,
                                        ALU.logical_shift_right))
                chain(dve.tensor_scalar(rs_a[:, :].bitcast(I32), rs_b[:, :].bitcast(I32), -1.0, float(0x5f3759df),
                                        ALU.mult, ALU.add))
                for _ in range(3):
                    chain(dve.tensor_tensor(rs_b[:, :], rs_a[:, :], rs_a[:, :], ALU.mult))
                    chain(dve.tensor_tensor(rs_b[:, :], rs_b[:, :], nhalf[:, :], ALU.mult))
                    chain(dve.scalar_tensor_tensor(out=rs_a[:, :], in0=rs_b[:, :], scalar=1.5, in1=rs_a[:, :],
                                                   op0=ALU.add, op1=ALU.mult))

            def lines_c(c):
                rs = spread(rs_a[:, :].rearrange("p (h o) -> p h o", o=1), 2, LINE)
                chain(dve.scalar_tensor_tensor(out=prodB[:, :, :], in0=prodA[:, :, :], scalar=SPLIT_UP, in1=rs,
                                               op0=ALU.mult, op1=ALU.mult))
                dve.wait_ge(featT_full, HP * c)
                chain(dve.tensor_copy(feat[:, :, 0:LINE], prodB[:, :, :]))
                dve.tensor_tensor(feat[:, :, LINE:2 * LINE], prodB[:, :, :], feat[:, :, 0:LINE], ALU.subtract)\
                    .then_inc(prodB_read, 1)
                dve.wait_ge(prodB_read, c + 1)
                f = feat[:, :, :].rearrange("p (s h) l -> p s h l", s=2)
                dve.tensor_copy(f[:, 0, :, 2 * LINE:4 * LINE], f[:, 0, :, 0:2 * LINE])
                dve.tensor_copy(f[:, 1, :, 2 * LINE:3 * LINE], f[:, 1, :, LINE:2 * LINE])
                dve.tensor_copy(f[:, 1, :, 3 * LINE:4 * LINE], f[:, 1, :, 0:LINE]).then_inc(feat_done, 1)

            def copy_feat(c, par, g):
                dve.wait_ge(featT_full, HP * c + g + 1)
                dve.tensor_copy(qkT[:, par, g, :, :].rearrange("p s n -> p (s n)"),
                                W[(g + 1) % 2][:, :].bitcast(FP16)).then_inc(featT_read, 1)

            def normalise(c, t):
                dve.wait_ge(outT_full, NT * c + t + 1)
                w = W[(t + 1) % 2][:, :].rearrange("p (h n) -> p h n", n=32)
                chain(dve.reciprocal(rden[:, t, :].rearrange("p (h o) -> p h o", o=1), w[:, :, DH:DH + 1]))
                dve.tensor_tensor(o_tok[:, t, :].rearrange("p (h d) -> p h d", d=DH), w[:, :, 0:DH],
                                  spread(rden[:, t, :].rearrange("p (h o) -> p h o", o=1), 2, DH), ALU.mult)\
                    .then_inc(outT_read, 1)

            def residual(c, par):
                dve.wait_ge(y_full, c + 1)
                dve.wait_ge(xres_done, c + 1)
                dve.tensor_tensor(ysum[:, :, :], W0[:, :].rearrange("p (t n) -> p t n", t=NT), xres[:, par, :, :],
                                  ALU.add).then_inc(y_read, 1)
                dve.wait_ge(y_read, c + 1)
                for t in range(NT):
                    ins = dve.bn_stats(stats[:, t, :], ysum[:, t, :])
                chain(ins)
                dve.sem_inc(parted, 1)
                for t in range(NT):
                    ins = dve.bn_aggr(meanvar[:, t, :], stats[:, t, :])
                chain(ins)
                dve.tensor_scalar(vareps[:, :], meanvar[:, :, 1], EPS, None, ALU.add).then_inc(var_done, 1)

            def norm_out(c, par):
                dve.wait_ge(rstd_done, c + 1)
                dve.wait_ge(x1_out[par], 16 * ((c - par) // 2) + 16)
                for t in range(NT):
                    ins = dve.tensor_scalar(x1[:, par, t, :], ysum[:, t, :], meanvar[:, t, 0:1], rstd[:, t:t + 1],
                                            ALU.subtract, ALU.mult)
                ins.then_inc(x1_done, 1)

            def split(c, par):
                dve.wait_ge(x1_done, c + 1)
                dve.wait_ge(rows_out[par], 2 * NT * 16 * ((c - par) // 2) + 16)
                h = xrow[:, par, :, 0, 0:P].bitcast(FP16)
                chain(dve.tensor_scalar(h[:, :, 0:P], x1[:, par, :, :], UP, None, ALU.mult))
                chain(dve.scalar_tensor_tensor(out=h[:, :, P:2 * P], in0=x1[:, par, :, :], scalar=UP,
                                               in1=h[:, :, 0:P], op0=ALU.mult, op1=ALU.subtract))
                dve.tensor_copy(xrow[:, par, :, 1, 0:P], xrow[:, par, :, 0, 0:P]).then_inc(split_done, 1)

            def choose(c, par):
                dve.wait_ge(logit_full, c + 1)
                dve.scalar_tensor_tensor(out=rt["logit"][:, :, :], in0=W1[:, 0:NT * NE].rearrange("p (t e) -> p t e", t=NT),
                                         scalar=1.0 / UP ** 2, in1=rb4[:, :, :], op0=ALU.mult, op1=ALU.add)\
                    .then_inc(logit_read, 1)
                dve.wait_ge(tanh_done, c + 1)
                prob, eq, cand, rest = (rt[n][:, :, :] for n in ("prob", "eq", "cand", "rest"))
                chain(dve.tensor_scalar(prob, prob, 0.5, 0.5, ALU.mult, ALU.add))
                for k, src in enumerate((prob, rest)):
                    if k:
                        chain(dve.scalar_tensor_tensor(out=rest, in0=one[:, 0], scalar=-4.0, in1=prob, op0=ALU.mult,
                                                       op1=ALU.add))
                    chain(dve.tensor_reduce(rmax[:, k, :], src, AX.X, ALU.max))
                    chain(dve.tensor_tensor(eq, src, per_expert(rmax[:, k, :]), ALU.is_equal))
                    chain(dve.tensor_tensor(cand, eq, iota_e[:, :, :], ALU.mult))
                    chain(dve.tensor_reduce(rmin[:, :], cand, AX.X, ALU.min))
                    chain(dve.tensor_tensor(one[:, k], cand, per_expert(rmin[:, :]), ALU.is_equal))
                dve.tensor_tensor(picks[:, :, :], one[:, 0], one[:, 1], ALU.add).then_inc(picks_done, 1)
                tail = xrow[:, par].rearrange("p t k w -> p k t w")
                dve.tensor_scalar(tail[:, :, :, P], rmax[:, :, :], 1.0 / (UP * H_UP), None, ALU.mult)
                chain(dve.tensor_copy(tail[:, :, :, P + 1].bitcast(I32), place_i[:, :, :]))
                dve.tensor_scalar(place_i[:, :, :], place_i[:, :, :], T, None, ALU.add)

            def per_expert(v):
                return spread(v.rearrange("p (t o) -> p t o", o=1), 2, NE)

            def slots(c, par):
                dve.wait_ge(rank_full, c + 1)
                slot = rt["slot"][:, :, :]
                chain(dve.tensor_tensor(slot, W1[:, 0:NT * NE].rearrange("p (t e) -> p t e", t=NT),
                                        spread(next_slot[:, :].rearrange("p (o e) -> p o e", o=1), 1, NT), ALU.add))
                dve.tensor_tensor(next_slot[:, :], next_slot[:, :], W1[:, NT * NE:(NT + 1) * NE], ALU.add)\
                    .then_inc(rank_read, 1)
                for k in range(2):
                    ins = dve.tensor_tensor(oneslot[:, k], one[:, k], slot, ALU.mult)
                chain(ins)
                chain(dve.tensor_reduce(slot_f[:, :, :], oneslot[:, :, :, :], AX.X, ALU.add))
                dve.tensor_copy(slot_i[:, par], slot_f[:, :, :]).then_inc(rows_ready, 1)

            def add_bias(c, par):
                dve.wait_ge(xT_full, c + 1)
                dve.tensor_tensor(xres[:, par, :, :], x_in[:, par, :, :],
                                  spread(bo_bc[:, :].rearrange("p (o n) -> p o n", o=1), 1, NT), ALU.add)\
                    .then_inc(xres_done, 1)

            copy_xT(0)
            lines_a(0)
            lines_b(0)
            lines_c(0)
            for g in range(HP):
                copy_feat(0, 0, g)
            add_bias(0, 0)

            def body(b, par, first, last):
                count[0] = 0
                if not last:
                    copy_xT(b + 1)
                if not first:
                    for t in range(NT):
                        normalise(b - 1, t)
                if not last:
                    lines_a(b + 1)
                    lines_b(b + 1)
                    lines_c(b + 1)
                if routes(b):
                    choose(b - 2, par)
                if not first:
                    residual(b - 1, 1 - par)
                if not last:
                    for g in range(HP):
                        copy_feat(b + 1, 1 - par, g)
                if routes(b):
                    slots(b - 2, par)
                if not first:
                    norm_out(b - 1, 1 - par)
                    split(b - 1, 1 - par)
                if not last:
                    add_bias(b + 1, 1 - par)
                base[0] = base[0] + count[0]
            per = 4 + (4 + 12 + 2) + 2 + 2 + 13 + 3
            base[0] = count[0]
            body(0, 0, True, False)
            body(1, 1, False, False)
            start = base[0]
            with dve.Fori(1, NB // 2 - 1) as i:
                base[0] = start + (i - 1) * (2 * per)
                body(2 * i, 0, False, False)
                assert count[0] == per, count[0]
                body(2 * i + 1, 1, False, False)
                assert count[0] == per
            base[0] = start + (NB // 2 - 2) * 2 * per
            body(NB - 2, 0, False, False)
            body(NB - 1, 1, False, True)
            count[0] = 0
            for t in range(NT):
                normalise(NB - 1, t)
            residual(NB - 1, 1)
            norm_out(NB - 1, 1)
            split(NB - 1, 1)
            for c in (NB - 2, NB - 1):
                choose(c, c % 2)
                slots(c, c % 2)


        block_scope.close()
        phase1.close()

        NX = NE + 1
        NSH = NTOK // UNIT
        NRT = 2 * NTOK // UNIT + NE
        NRING = 4
        phase2 = ctx.enter_context(ExitStack())

        def sb2(name, shape, dt=FP32):
            return phase2.enter_context(nc.sbuf_tensor(name, shape, dt))

        w_raw = sb2("w_raw", [P, NX, 6, P])
        w_T = sb2("w_T", [P, NX, 2, 6, P], FP16)
        sch = {n: sb2("sch_" + n, [P, NE]) for n in ("count", "units", "end", "gap")}
        sch_i = sb2("sch_i", [P, NE], I32)
        slot_end = sb2("slot_end", [P, NE], I32)
        unit_i = sb2("unit_i", [P, NRT], I32)
        unit_f = sb2("unit_f", [P, NRT])
        past = sb2("past", [P, NRT, NE])
        past_gap = sb2("past_gap", [P, NRT, NE])
        unit_sum = sb2("unit_sum", [P, 2, NRT])
        unit_expert = sb2("unit_expert", [P, NRT], I32)
        unit_row = sb2("unit_row", [P, NRT], I32)
        x1_in = sb2("x1_in", [P, NRING, 2, P])
        rows = sb2("rows", [P, NRING, 2, ROW])
        xT_sh = sb2("xT_sh", [P, NRING, 2, UNIT], FP16)
        xT_rt = sb2("xT_rt", [P, 2, 2, UNIT], FP16)
        th = sb2("th", [P, 2, 2 * UNIT])
        gated = sb2("gated", [P, 2, 2 * UNIT])
        hid = sb2("hid", [P, 2, 2 * UNIT])
        hid16 = sb2("hid16", [P, 2, 2, 2 * UNIT], FP16)
        y = sb2("y", [P, NRING, 2, P])
        acc = sb2("acc", [P, NTOK // P, P])
        z = sb2("z", [P, 2, 2, NT, P])
        zsum = sb2("zsum", [P, 2, NT, P])
        tot = sb2("tot", [P, 2, NT, P])
        stats2 = sb2("stats2", [P, NT, 6])
        meanvar2 = sb2("meanvar2", [P, 2, NT, 2])
        vareps2 = sb2("vareps2", [P, NT])
        rstd2 = sb2("rstd2", [P, 2, NT])
        shift2 = sb2("shift2", [P, 2, NT])
        res = sb2("res", [P, 2, NT, P])

        w2_in = [sem(f"w2_in{e}") for e in range(NX)]
        w2T_full = sem("w2T_full"); w2T_hi = sem("w2T_hi"); w2T_lo = sem("w2T_lo")
        consts2 = sem("consts2"); slot_end_done = sem("slot_end_done"); table_done = sem("table_done")
        pads_out = sem("pads_out")
        sh_in = [sem(f"sh_in{r}") for r in range(NRING)]
        rt_in = [sem(f"rt_in{r}") for r in range(NRING)]
        xT2_full = sem("xT2_full"); xT2_read = sem("xT2_read")
        gu_full = sem("gu_full"); gate_tanh = sem("gate_tanh"); hid_done = sem("hid_done"); hi_done = sem("hi_done")
        lo_done = sem("lo_done"); down_full = sem("down_full"); acc_done = sem("acc_done")
        y_ready = sem("y_ready"); z_out = [sem(f"z_out{r}") for r in range(NRING)]
        z_in = [sem("z_in0"), sem("z_in1")]; zsum_done = sem("zsum_done"); tot_done = sem("tot_done")
        var2_done = sem("var2_done"); rstd2_done = sem("rstd2_done"); shift_done = sem("shift_done")
        res_done = sem("res_done"); res_out = [sem("res_out0"), sem("res_out1")]
        step2 = sem("step2")
        halves = "(a p) d -> p a d"
        w_src = [[(Wg_s, Wu_s, Wd_s)[k].rearrange(halves if k < 2 else "p (a d) -> p a d",
                                                  **({"p": P} if k < 2 else {"d": P})) for k in range(3)]]
        for e in range(NE):
            w_src.append([Wg[e].rearrange(halves, p=P), Wu[e].rearrange(halves, p=P),
                          Wd[e].rearrange("p (a d) -> p a d", d=P)])

        def over_units(eng, body):
            R = NRING
            for u in range(R):
                body(u, u, u, 0, True)
            with eng.Fori(1, NSH // R) as i:
                for r in range(R):
                    body(R * i + r, R * i + r, r, i, True)
            for u in range(R):
                body(NSH + u, u, u, 0, False)
            with eng.Fori(1, NRT // R) as i:
                for r in range(R):
                    body(NSH + R * i + r, R * i + r, r, i, False)
        assert NSH % NRING == 0 and NRT % NRING == 0

        block2 = ctx.enter_context(nc.Block())

        @block2.sync
        def _(sp):
            for e in range(NX):
                for k in range(3):
                    sp.dma_start(w_raw[:, e, 2 * k:2 * k + 2, :], w_src[e][k]).then_inc(w2_in[e], 16)

            def body(u, n, r, i, shared):
                if shared:
                    if not isinstance(i, int):
                        sp.wait_ge(acc_done, n - NRING + 1)
                    half = r % 2
                    b = (n - half) // 2
                    sp.dma_start(xT_sh[:, r], x1T_dram[bass.ds(b, 1), :, :, half * UNIT:(half + 1) * UNIT]
                                 .rearrange("a p s n -> p (a s) n")).then_inc(sh_in[r], 16)
                    sp.dma_start(x1_in[:, r], x1_dram[bass.ds(b, 1), half * UNIT:(half + 1) * UNIT, :]
                                 .rearrange("o (a p) d -> p (o a) d", p=P)).then_inc(sh_in[r], 16)
                    return
                if isinstance(u, int) and u == NSH:
                    sp.wait_ge(slot_end_done, 1)
                    for e in range(NE):
                        at = sp.value_load(slot_end[0:1, e:e + 1], min_val=e * CAP, max_val=e * CAP + NTOK)
                        sp.dma_start(rows_dram[bass.ds(at, UNIT)].rearrange("(a p) w -> p a w", p=P), pad_rows[:, :, :])\
                            .then_inc(pads_out, 16)
                    sp.wait_ge(pads_out, 16 * NE)
                    sp.wait_ge(table_done, 1)
                if not isinstance(i, int):
                    sp.wait_ge(z_out[r], 2 * 16 * i)
                at = sp.value_load(unit_row[0:1, bass.ds(n, 1)], min_val=0, max_val=TAIL)
                sp.dma_start(rows[:, r], rows_dram[bass.ds(at, UNIT)].rearrange("(a p) w -> p a w", p=P))\
                    .then_inc(rt_in[r], 16)
            over_units(sp, body)
            for r in range(NRING):
                sp.wait_ge(z_out[r], 2 * 16 * (NRT // NRING))

            def load_z(b, par):
                for k in range(2):
                    sp.dma_start(z[:, par, k], z_dram[bass.ds(b * T + k * NTOK, T)].rearrange("(t p) d -> p t d", p=P))\
                        .then_inc(z_in[par], 16)
            load_z(0, 0)
            load_z(1, 1)

            def finish(b, par, more):
                sp.wait_ge(res_done, b + 1)
                sp.dma_start(out[bass.ds(b, 1)].rearrange("a (t p) d -> p (a t) d", p=P), res[:, par])\
                    .then_inc(res_out[par], 16)
                if more:
                    sp.wait_ge(zsum_done, b + 1)
                    load_z(b + 2, par)
            with sp.Fori(0, NB // 2 - 1) as i:
                finish(2 * i, 0, True)
                finish(2 * i + 1, 1, True)
            finish(NB - 2, 0, False)
            finish(NB - 1, 1, False)
            for par in range(2):
                sp.wait_ge(res_out[par], 16 * NB // 2)

        @block2.gpsimd
        def _(pool):
            pool.iota(unit_i[:, :], pattern=[[1, NRT]], base=0, channel_multiplier=0).then_inc(consts2, 1)

            def body(u, n, r, i, shared):
                if shared:
                    return
                pool.wait_ge(y_ready, n + 1)
                pool.sem_inc(parted, 1)
                for a in range(2):
                    pool.indirect_dma_start(
                        out=z_dram, in_=y[:, r, a, :], in_offset=None,
                        out_offset=bass.IndirectOffsetOnAxis(ap=rows[:, r, a, P + 1:P + 2].bitcast(I32), axis=0),
                        bounds_check=2 * NTOK - 1, oob_is_err=False).then_inc(z_out[r], 16)
            for u in range(NRING):
                body(NSH + u, u, u, 0, False)
            with pool.Fori(1, NRT // NRING) as i:
                for r in range(NRING):
                    body(NSH + NRING * i + r, NRING * i + r, r, i, False)

            def finish(b, par, i):
                pool.wait_ge(z_in[par], 32 * (i + 1))
                if not isinstance(i, int):
                    pool.wait_ge(tot_done, b - 1)
                pool.tensor_tensor(zsum[:, par], z[:, par, 0], z[:, par, 1], ALU.add).then_inc(zsum_done, 1)
                pool.wait_ge(var2_done, b + 1)
                pool.tensor_tensor(rstd2[:, par, :], vareps2[:, :], minus_half[:, :], ALU.pow).then_inc(rstd2_done, 1)
            finish(0, 0, 0)
            finish(1, 1, 0)
            with pool.Fori(1, NB // 2) as i:
                finish(2 * i, 0, i)
                finish(2 * i + 1, 1, i)

        @block2.tensor
        def _(pe):
            for e in range(NX):
                pe.wait_ge(w2_in[e], 48)
                for h, (a, n) in enumerate(((0, 4), (4, 2))):
                    if e:
                        pe.wait_ge(w2T_lo, 2 * e + h - 1)
                    for k in range(n):
                        mm = pe.transpose(W[h][:, k * P:(k + 1) * P], w_raw[:, e, a + k, :], ident[:, :])
                    mm.then_inc(w2T_full, 1)
            pe.wait_ge(w2T_lo, 2 * NX)

            def gate_up(u, r, xT, e):
                if not (isinstance(u, int) and u < 2):
                    pe.wait_ge(hid_done, u - 1)
                for k in range(4):
                    for n, (a, w) in enumerate(((0, 0), (1, 0), (0, 1))):
                        mm = pe.matmul(S[r % 2][:, k * UNIT:(k + 1) * UNIT], weights(e, w, k), xT[:, a, :],
                                       start=(n == 0), stop=(n == 2))
                mm.then_inc(gu_full, 1)

            def weights(e, w, k):
                if isinstance(e, int):
                    return w_T[:, e, w, k, :]
                return w_T[:, bass.ds(e, 1), w, k, :].rearrange("p o n -> p (o n)")

            def down(u, r, e, shared):
                pe.wait_ge(lo_done, u + 1)
                if isinstance(u, int) and u < NSH + 2:
                    if u >= 2:
                        pe.wait_ge(acc_done, u - 1)
                elif not shared:
                    pe.wait_ge(y_ready, u - NSH - 1)
                else:
                    pe.wait_ge(acc_done, u - 1)
                par = r % 2
                for a in range(2):
                    n = 0
                    for k in range(2):
                        for h, w in ((0, 0), (0, 1), (1, 0)):
                            mm = pe.matmul(O[par][:, a * P:(a + 1) * P],
                                           hid16[:, par, h, k * UNIT + a * P:k * UNIT + (a + 1) * P],
                                           weights(e, w, 4 + k), start=(n == 0), stop=(n == 5))
                            n += 1
                mm.then_inc(down_full, 1)

            def transposes(n, r, i):
                pe.wait_ge(rt_in[r], 16 * (i + 1))
                if not (isinstance(n, int) and n < 2):
                    pe.wait_ge(xT2_read, n - 1)
                w = W[r % 2][:, 0:UNIT].bitcast(FP16).rearrange("p (s m) -> p s m", s=2)
                for s in range(2):
                    for a in range(2):
                        src = rows[:, r, a, s * P // 2:(s + 1) * P // 2].bitcast(FP16)
                        mm = pe.transpose(w[:, s, a * P:(a + 1) * P], src, ident16[:, :])
                mm.then_inc(xT2_full, 1)

            def body(u, n, r, i, shared):
                first = isinstance(n, int) and n == 0
                if shared:
                    pe.wait_ge(sh_in[r], 32 * (i + 1))
                    gate_up(u, r, xT_sh[:, r], 0)
                    if not first:
                        down(u - 1, r - 1, 0, True)
                    return
                if first:
                    pe.wait_ge(table_done, 1)
                    transposes(0, 0, 0)
                    down(u - 1, r - 1, 0, True)
                expert = pe.value_load(unit_expert[0:1, bass.ds(n, 1)], min_val=1, max_val=NE)
                pe.wait_ge(xT2_read, n + 1)
                gate_up(u, r, xT_rt[:, r % 2], expert)
                if not first:
                    before = pe.value_load(unit_expert[0:1, bass.ds(n - 1, 1)], min_val=1, max_val=NE)
                    down(u - 1, r - 1, before, False)
                if not (isinstance(n, int) and n == NRT - 1):
                    nxt = (r + 1) % NRING
                    transposes(n + 1, nxt, i if nxt else i + 1)
            R = NRING
            for u in range(R):
                body(u, u, u, 0, True)
            with pe.Fori(1, NSH // R) as i:
                for r in range(R):
                    body(R * i + r, R * i + r, r, i, True)
            for u in range(R):
                body(NSH + u, u, u, 0, False)
            with pe.Fori(1, NRT // R - 1) as i:
                for r in range(R):
                    body(NSH + R * i + r, R * i + r, r, i, False)
            for r in range(R):
                n = NRT - R + r
                body(NSH + n, n, r, NRT // R - 1, False)
            last = pe.value_load(unit_expert[0:1, NRT - 1:NRT], min_val=1, max_val=NE)
            down(NSH + NRT - 1, R - 1, last, False)

        @block2.scalar
        def _(act):
            for e in range(NX):
                for h, (a, n) in enumerate(((0, 4), (4, 2))):
                    act.wait_ge(w2T_full, 2 * e + h + 1)
                    act.activation(w_T[:, e, 0, a:a + n, :].rearrange("p k n -> p (k n)"), W[h][:, 0:n * P], ACT.Copy,
                                   scale=UP).then_inc(w2T_hi, 1)

            def send(n, r, i):
                act.wait_ge(down_full, NSH + n + 1)
                act.wait_ge(rt_in[r], 16 * (i + 1))
                for a in range(2):
                    ins = act.activation(y[:, r, a, :], O[r % 2][:, a * P:(a + 1) * P], ACT.Copy,
                                         scale=rows[:, r, a, P:P + 1])
                ins.then_inc(y_ready, 1)

            def body(u, n, r, i, shared):
                act.wait_ge(gu_full, u + 1)
                if not (isinstance(u, int) and u < 2):
                    act.wait_ge(hid_done, u - 1)
                act.activation(th[:, r % 2, :], S[r % 2][:, 0:2 * UNIT], ACT.Tanh, scale=0.5 / UP ** 2)\
                    .then_inc(gate_tanh, 1)
                if not shared and not (isinstance(n, int) and n == 0):
                    send(n - 1, (r - 1) % NRING, i if r else i - 1)
                act.wait_ge(hid_done, u + 1)
                if not (isinstance(u, int) and u < 2):
                    act.wait_ge(down_full, u - 1)
                act.copy(hid16[:, r % 2, 0, :], hid[:, r % 2, :]).then_inc(hi_done, 1)

            over_units(act, body)
            send(NRT - 1, NRING - 1, NRT // NRING - 1)

            def finish(b, par, i):
                act.wait_ge(shift_done, b + 1)
                if not isinstance(i, int):
                    act.wait_ge(res_out[par], 16 * i)
                for t in range(NT):
                    ins = act.activation(res[:, par, t, :], tot[:, par, t, :], ACT.Identity, scale=rstd2[:, par, t:t + 1],
                                         bias=shift2[:, par, t:t + 1])
                ins.then_inc(res_done, 1)
            finish(0, 0, 0)
            finish(1, 1, 0)
            with act.Fori(1, NB // 2) as i:
                finish(2 * i, 0, i)
                finish(2 * i + 1, 1, i)

        @block2.vector
        def _(dve):
            count = [0]
            base = [0]

            def chain(ins):
                ins.then_inc(step2, 1)
                count[0] += 1
                dve.wait_ge(step2, base[0] + count[0])

            dve.wait_ge(consts2, 1)
            N, U, E, G = (sch[n][:, :] for n in ("count", "units", "end", "gap"))
            dve.tensor_copy(slot_end[:, :], next_slot[:, :]).then_inc(slot_end_done, 1)
            dve.tensor_copy(unit_f[:, :], unit_i[:, :])
            for e in range(NE):
                ins = dve.tensor_scalar(N[:, e:e + 1], next_slot[:, e:e + 1], float(UNIT - 1 - e * CAP), None, ALU.add)
            chain(ins)
            chain(dve.tensor_copy(sch_i[:, :], N))
            chain(dve.tensor_scalar(sch_i[:, :], sch_i[:, :], UNIT.bit_length() - 1, None, ALU.logical_shift_right))
            chain(dve.tensor_copy(U, sch_i[:, :]))
            dve.tensor_scalar(G, U, -float(UNIT), float(CAP), ALU.mult, ALU.add)
            chain(dve.tensor_copy(E[:, 0:1], U[:, 0:1]))
            for e in range(1, NE):
                chain(dve.tensor_tensor(E[:, e:e + 1], E[:, e - 1:e], U[:, e:e + 1], ALU.add))

            def by_unit(v):
                return spread(v.rearrange("p (o e) -> p o e", o=1), 1, NRT)
            chain(dve.tensor_tensor(past[:, :, :], spread(unit_f[:, :].rearrange("p (n o) -> p n o", o=1), 2, NE),
                                    by_unit(E), ALU.is_ge))
            chain(dve.tensor_tensor(past_gap[:, :, :], past[:, :, :], by_unit(G), ALU.mult))
            dve.tensor_reduce(unit_sum[:, 0, :], past[:, :, :], AX.X, ALU.add)
            chain(dve.tensor_reduce(unit_sum[:, 1, :], past_gap[:, :, :], AX.X, ALU.add))
            dve.tensor_scalar(unit_expert[:, :], unit_sum[:, 0, :], 1.0, float(NE), ALU.add, ALU.min)
            chain(dve.scalar_tensor_tensor(out=past_gap[:, :, 0], in0=unit_f[:, :], scalar=float(UNIT),
                                           in1=unit_sum[:, 1, :], op0=ALU.mult, op1=ALU.add))
            dve.tensor_scalar(unit_row[:, :], past_gap[:, :, 0], float(TAIL), None, ALU.min).then_inc(table_done, 1)

            for e in range(NX):
                for h, (a, n) in enumerate(((0, 4), (4, 2))):
                    dve.wait_ge(w2T_hi, 2 * e + h + 1)
                    dve.scalar_tensor_tensor(out=w_T[:, e, 1, a:a + n, :].rearrange("p k n -> p (k n)"), in0=W[h][:, 0:n * P],
                                             scalar=UP, in1=w_T[:, e, 0, a:a + n, :].rearrange("p k n -> p (k n)"),
                                             op0=ALU.mult, op1=ALU.subtract).then_inc(w2T_lo, 1)

            def copy_xT(n, r):
                dve.wait_ge(xT2_full, n + 1)
                if not (isinstance(n, int) and n < 2):
                    dve.wait_ge(gu_full, NSH + n - 1)
                dve.tensor_copy(xT_rt[:, r % 2].rearrange("p s m -> p (s m)"), W[r % 2][:, 0:UNIT].bitcast(FP16))\
                    .then_inc(xT2_read, 1)

            def add_shared(n, r):
                dve.wait_ge(down_full, n + 1)
                dst = acc[:, bass.ds(2 * n, 2), :] if not isinstance(n, int) else acc[:, 2 * n:2 * n + 2, :]
                dve.scalar_tensor_tensor(out=dst.rearrange("p a d -> p (a d)"), in0=O[r % 2][:, 0:UNIT],
                                         scalar=1.0 / (UP * H_UP), in1=x1_in[:, r].rearrange("p a d -> p (a d)"),
                                         op0=ALU.mult, op1=ALU.add).then_inc(acc_done, 1)

            def body(u, n, r, i, shared):
                par = r % 2
                first = isinstance(n, int) and n == 0
                dve.wait_ge(gate_tanh, u + 1)
                if not (isinstance(u, int) and u < 2):
                    dve.wait_ge(hi_done, u - 1)
                dve.scalar_tensor_tensor(out=gated[:, par, :], in0=th[:, par, :], scalar=1.0, in1=S[par][:, 0:2 * UNIT],
                                         op0=ALU.add, op1=ALU.mult).then_inc(gated_done, 1)
                dve.wait_ge(gated_done, u + 1)
                dve.scalar_tensor_tensor(out=hid[:, par, :], in0=gated[:, par, :], scalar=0.5 * H_UP / UP ** 4,
                                         in1=S[par][:, 2 * UNIT:4 * UNIT], op0=ALU.mult, op1=ALU.mult)\
                    .then_inc(hid_done, 1)
                if shared and not first:
                    add_shared(n - 1, r - 1 if r else NRING - 1)
                if not shared:
                    if first:
                        add_shared(NSH - 1, NRING - 1)
                    if not (isinstance(n, int) and n == NRT - 1):
                        copy_xT(n + 1, r + 1)
                dve.wait_ge(hi_done, u + 1)
                dve.tensor_tensor(hid16[:, par, 1, :], hid[:, par, :], hid16[:, par, 0, :], ALU.subtract)\
                    .then_inc(lo_done, 1)
            gated_done = sem("gated_done")
            R = NRING
            for u in range(R):
                body(u, u, u, 0, True)
            with dve.Fori(1, NSH // R) as i:
                for r in range(R):
                    body(R * i + r, R * i + r, r, i, True)
            copy_xT(0, 0)
            for u in range(R):
                body(NSH + u, u, u, 0, False)
            with dve.Fori(1, NRT // R - 1) as i:
                for r in range(R):
                    body(NSH + R * i + r, R * i + r, r, i, False)
            for r in range(R):
                n = NRT - R + r
                body(NSH + n, n, r, NRT // R - 1, False)

            at = count[0]

            def finish(b, par, i):
                base[0], count[0] = at + PER2 * b, 0
                dve.wait_ge(zsum_done, b + 1)
                if not isinstance(i, int):
                    dve.wait_ge(res_done, b - 1)
                src = acc[:, NT * b:NT * (b + 1), :] if isinstance(b, int) else acc[:, bass.ds(NT * b, NT), :]
                dve.tensor_tensor(tot[:, par], src, zsum[:, par], ALU.add).then_inc(tot_done, 1)
                dve.wait_ge(tot_done, b + 1)
                for t in range(NT):
                    ins = dve.bn_stats(stats2[:, t, :], tot[:, par, t, :])
                chain(ins)
                dve.sem_inc(parted, 1)
                for t in range(NT):
                    ins = dve.bn_aggr(meanvar2[:, par, t, :], stats2[:, t, :])
                chain(ins)
                dve.tensor_scalar(vareps2[:, :], meanvar2[:, par, :, 1], EPS, None, ALU.add).then_inc(var2_done, 1)
                dve.wait_ge(rstd2_done, b + 1)
                dve.scalar_tensor_tensor(out=shift2[:, par, :], in0=meanvar2[:, par, :, 0], scalar=-1.0,
                                         in1=rstd2[:, par, :], op0=ALU.mult, op1=ALU.mult).then_inc(shift_done, 1)
                assert count[0] == PER2
            PER2 = 2
            finish(0, 0, 0)
            finish(1, 1, 0)
            with dve.Fori(1, NB // 2) as i:
                finish(2 * i, 0, i)
                finish(2 * i + 1, 1, i)


_INS = ["L0_attn_x", "L0_attn_W1_q", "L0_attn_W2_q", "L0_attn_W1_k", "L0_attn_W2_k", "L0_attn_Wv", "L0_attn_bv",
        "L0_attn_Wo", "L0_attn_bo", "L0_ffn_Wg_s", "L0_ffn_Wu_s", "L0_ffn_Wd_s", "L0_ffn_Wg", "L0_ffn_Wu",
        "L0_ffn_Wd", "L0_ffn_Wr", "L0_ffn_rb"]


def kernel(**inputs):
    import numpy as np
    import concourse.bacc as bacc
    from concourse.bass_utils import run_bass_kernel_spmd

    nc = bacc.Bacc("TRN2", target_bir_lowering=False, num_devices=1)
    arrays, args = {}, []
    for name in _INS:
        a = np.ascontiguousarray(inputs[name])
        arrays[f"in_{name}"] = a
        args.append(nc.dram_tensor(f"in_{name}", a.shape, mybir.dt.from_np(a.dtype), kind="ExternalInput").ap())
    shape = inputs["L0_attn_x"].shape
    out = nc.dram_tensor("out_0", shape, FP32, kind="ExternalOutput").ap()
    block_program(nc, *args, out)
    return run_bass_kernel_spmd(nc, [arrays], core_ids=[0]).results[0]["out_0"]
```

```python
import concourse.bass as bass
from concourse import mybir
from contextlib import ExitStack

FP32 = mybir.dt.float32
FP16 = mybir.dt.float16
I32 = mybir.dt.int32
ALU = mybir.AluOpType
ACT = mybir.ActivationFunctionType
AX = mybir.AxisListType

P = 128
T = 512
NT = T // P
H = 16
DH = P // H
HP = H // 4
LINE = 6
FEAT = 32
HH = 2 * H
SPLIT_UP = 1024.0
SCALE = 6.0 ** -0.5
NE = 8
FF = 256
EPS = 1e-5
UP = 64.0
H_UP = 8.0
ROW = P + 2
UNIT = 2 * P

CHUNK = 1024
NCHUNK = 5
PIECES = {
    (0, 0): (0, 0), (0, 3): (0, 512), (0, 1): (0, 640),
    (1, 0): (1, 0), (1, 3): (1, 512), (1, 1): (1, 640),
    (0, 2): (2, 0), (2, 0): (2, 512), (1, 2): (2, 256),
    (2, 3): (3, 0), (2, 1): (3, 128), (3, 0): (3, 512),
    (2, 2): (4, 512), (3, 3): (4, 0), (3, 1): (4, 128), (3, 2): (4, 768),
}
BANK_MATE = {(1, 2): (0, 2), (3, 2): (2, 2)}
SQUARES = {
    0: [(0, 1, 128), (512, 2, 128)],
    1: [(0, 1, 128), (512, 2, 128)],
    2: [(0, 3, 256)],
    3: [(0, 2, 128), (512, 1, 128)],
    4: [(0, 2, 128), (512, 2, 256)],
}


def spread(ap, dim, n):
    shape = list(ap.shape)
    shape[dim] = n
    return ap.broadcast_to(shape)


def block_program(nc, x, W1_q, W2_q, W1_k, W2_k, Wv, bv, Wo, bo, Wg_s, Wu_s, Wd_s, Wg, Wu, Wd, Wr, rb, out):
    NB = x.shape[0]
    ctx = ExitStack()
    with ctx:
        def sb(name, shape, dt=FP32):
            return ctx.enter_context(nc.sbuf_tensor(name, shape, dt))

        def pb(name, shape, dt=FP32):
            return ctx.enter_context(nc.psum_tensor(name, shape, dt))

        def sem(name):
            return ctx.enter_context(nc.semaphore(name))

        phase1 = ExitStack()

        def sb1(name, shape, dt=FP32):
            return phase1.enter_context(nc.sbuf_tensor(name, shape, dt))

        ident = sb("ident", [P, P])
        ident16 = sb("ident16", [P, P], FP16)
        next_slot = sb("next_slot", [P, NE])
        pad_rows = sb("pad_rows", [P, 2, ROW])
        minus_half = sb("minus_half", [P, 4])
        NX = NE + 1
        w_raw = sb("w_raw", [P, NX, 6, P])
        xrow = sb("xrow", [P, 2, NT, 2, ROW])
        slot_i = sb("slot_i", [P, 2, 2, NT], I32)
        w_nat = sb1("w_nat", [P, 8, P])
        w_allT = sb1("w_allT", [P, 3 * P])
        w_prevT = sb1("w_prevT", [P, P])
        w_oT = sb1("w_oT", [P, P])
        bv_col = sb1("bv_col", [P, 1])
        bv_cols = sb1("bv_cols", [P, P])
        bo_bc = sb1("bo_bc", [P, P])
        x_in = sb1("x_in", [P, 2, NT, P])
        xres = sb1("xres", [P, 2, NT, P])
        xT = sb1("xT", [P, T + 1])
        p12 = sb1("p12", [P, 2, 2, NT, H, 4])
        v_aug = sb1("v_aug", [P, 2, NT, H, 32])
        prodA = sb1("prodA", [P, NT * HH, LINE])
        prodB = sb1("prodB", [P, NT * HH, LINE])
        nrm = sb1("nrm", [P, NT * HH])
        nhalf = sb1("nhalf", [P, NT * HH])
        rs_a = sb1("rs_a", [P, NT * HH])
        rs_b = sb1("rs_b", [P, NT * HH])
        feat = sb1("feat", [P, NT * HH, FEAT], FP16)
        qkT = sb1("qkT", [P, 2, HP, 2, T], FP16)
        probs = sb1("probs", [P, 2, NCHUNK, CHUNK])
        oT_raw = sb1("oT_raw", [P, HP, T])
        rden = sb1("rden", [P, NT, H])
        o_tok = sb1("o_tok", [P, NT, P])
        oT = sb1("oT", [P, T])
        ysum = sb1("ysum", [P, NT, P])
        stats = sb1("stats", [P, NT, 6])
        meanvar = sb1("meanvar", [P, NT, 2])
        vareps = sb1("vareps", [P, NT])
        rstd = sb1("rstd", [P, NT])
        x1 = sb1("x1", [P, 2, NT, P])
        x1T = sb1("x1T", [P, 2, 2, T], FP16)
        wr_raw = sb1("wr_raw", [NE, P])
        wr_T = sb1("wr_T", [P, 2, NE], FP16)
        rb_bc = sb1("rb_bc", [P, NE])
        rb4 = sb1("rb4", [P, NT, NE])
        iota_i = sb1("iota_i", [P, NT, NE], I32)
        iota_e = sb1("iota_e", [P, NT, NE])
        tri = sb1("tri", [P, P], FP16)
        ones16 = sb1("ones16", [P, P], FP16)
        picks = sb1("picks", [P, NT, NE], FP16)
        rt = {n: sb1("rt_" + n, [P, NT, NE]) for n in ("logit", "prob", "eq", "cand", "rest", "slot")}
        one = sb1("one", [P, 2, NT, NE])
        oneslot = sb1("oneslot", [P, 2, NT, NE])
        rmax = sb1("rmax", [P, 2, NT])
        rmin = sb1("rmin", [P, NT])
        slot_f = sb1("slot_f", [P, 2, NT])
        place_i = sb1("place_i", [P, 2, NT], I32)
        NTOK = NB * T
        CAP = NTOK + UNIT
        TAIL = NE * CAP
        x1_dram = nc.dram_tensor("x1_scratch", (NB, T, P), FP32).ap()
        x1T_dram = nc.dram_tensor("x1T_scratch", (NB, P, 2, T), FP16).ap()
        rows_dram = nc.dram_tensor("rows_scratch", (TAIL + UNIT, ROW), FP32).ap()
        z_dram = nc.dram_tensor("z_scratch", (2 * NTOK, P), FP32).ap()

        S = [pb(f"S{i}", [P, CHUNK]) for i in range(2)]
        O = [pb(f"O{i}", [P, T]) for i in range(2)]
        W0 = pb("W0", [P, T])
        W1 = pb("W1", [P, T])
        W = [W0, W1]

        wts_in = sem("wts_in"); consts = sem("consts"); xin_in = [sem("xin_in0"), sem("xin_in1")]
        wT_full = sem("wT_full"); wT_read = sem("wT_read")
        xT_full = sem("xT_full"); xT_read = sem("xT_read")
        pts_full = sem("pts_full"); pts_read = sem("pts_read"); val_full = sem("val_full"); val_read = sem("val_read")
        prodB_done = sem("prodB_done"); prodB_read = sem("prodB_read")
        feat_done = sem("feat_done"); featT_full = sem("featT_full"); featT_read = sem("featT_read")
        s_full = sem("s_full"); s_exp = sem("s_exp"); masked = sem("masked"); pv_done = sem("pv_done")
        o_read = sem("o_read")
        outT_full = sem("outT_full"); outT_read = sem("outT_read")
        oT_full = sem("oT_full"); oT_read = sem("oT_read")
        y_full = sem("y_full"); y_read = sem("y_read")
        var_done = sem("var_done"); rstd_done = sem("rstd_done")
        x1_done = sem("x1_done"); x1_out = [sem("x1_out0"), sem("x1_out1")]
        dve_step = sem("dve_step"); pool_step = sem("pool_step")
        xres_done = sem("xres_done"); parted = sem("parted"); pad_done = sem("pad_done"); split_done = sem("split_done")
        x1T_full = sem("x1T_full"); x1T_read = sem("x1T_read"); x1T_out = [sem("x1T_out0"), sem("x1T_out1")]
        logit_full = sem("logit_full"); logit_read = sem("logit_read"); tanh_done = sem("tanh_done")
        picks_done = sem("picks_done"); rank_full = sem("rank_full"); rank_read = sem("rank_read")
        rows_ready = sem("rows_ready"); rows_out = [sem("rows_out0"), sem("rows_out1")]; mate_done = sem("mate_done"); bv_spread = sem("bv_spread")

        loads = [
            (w_nat[0:64, 0, :], W1_q[:, 0:P]), (w_nat[64:128, 0, :], W1_k),
            (w_nat[0:64, 1, :], W2_q[:, 0:P]), (w_nat[64:128, 1, :], W2_k),
            (w_nat[:, 2, :], Wv), (w_nat[0:64, 3, :], W1_q[:, P:2 * P]), (w_nat[64:128, 3, :], W2_q[:, P:2 * P]),
            (w_nat[:, 4, :], Wo),
            (bv_col[:, :], bv.rearrange("(p o) -> p o", o=1)),
            (bo_bc[:, :], bo.partition_broadcast(P)), (wr_raw[:, :], Wr), (rb_bc[:, :], rb.partition_broadcast(P)),
        ]

        halves = "(a p) d -> p a d"
        w_src = [[(Wg_s, Wu_s, Wd_s)[k].rearrange(halves if k < 2 else "p (a d) -> p a d",
                                                  **({"p": P} if k < 2 else {"d": P})) for k in range(3)]]
        for e in range(NE):
            w_src.append([Wg[e].rearrange(halves, p=P), Wu[e].rearrange(halves, p=P),
                          Wd[e].rearrange("p (a d) -> p a d", d=P)])
        w2_in = [sem(f"w2_in{e}") for e in range(NX)]

        CONSTS = 11 + NE
        PEEL = 4

        def over_batches(eng, body):
            body(0, 0, True, False)
            for b in range(1, PEEL):
                body(b, b % 2, False, False)
            with eng.Fori(PEEL // 2, NB // 2 - 1) as i:
                body(2 * i, 0, False, False)
                body(2 * i + 1, 1, False, False)
            body(NB - 2, 0, False, False)
            body(NB - 1, 1, False, True)

        def routes(b):
            return not (isinstance(b, int) and b < 2)

        def sends(b):
            return not (isinstance(b, int) and b < 3)

        def ahead(b):
            return not (isinstance(b, int) and b + 2 >= NB)

        def dispatch(pool, c, par, tiles):
            if tiles[0] == 0:
                pool.wait_ge(rows_ready, c + 1)
                pool.sem_inc(parted, 1)
            for t in tiles:
                for k in range(2):
                    pool.indirect_dma_start(
                        out=rows_dram, in_=xrow[:, par, t, k, :], in_offset=None,
                        out_offset=bass.IndirectOffsetOnAxis(ap=slot_i[:, par, k, t:t + 1], axis=0),
                        bounds_check=TAIL - 1, oob_is_err=False).then_inc(rows_out[par], 16)

        def products(dst, many, one):
            d = dst[:, :, :].rearrange("p (s h) l -> p s h l", s=2)
            q_many, k_many = (p12[:, many, s].rearrange("p t h c -> p (t h) c") for s in range(2))
            q_one, k_one = (p12[:, one, s].rearrange("p t h c -> p (t h) c") for s in range(2))
            for i, l0, n in ((0, 0, 3), (1, 3, 2), (2, 5, 1)):
                yield d[:, 0, :, l0:l0 + n], q_many[:, :, i + 1:4], spread(q_one[:, :, i:i + 1], 2, n)
            for j, l0, n in ((1, 0, 1), (2, 1, 2), (3, 3, 3)):
                yield d[:, 1, :, l0:l0 + n], spread(k_many[:, :, j:j + 1], 2, n), k_one[:, :, 0:n]

        block_scope = ExitStack()
        block = block_scope.enter_context(nc.Block())

        @block.sync
        def _(sp):
            for dst, src in loads:
                sp.dma_start(dst, src).then_inc(wts_in, 16)
            for par in range(2):
                sp.sem_inc(x1_out[par], 16)
                sp.sem_inc(x1T_out[par], 16)
            for e in range(NX):
                for k in range(3):
                    sp.dma_start(w_raw[:, e, 2 * k:2 * k + 2, :], w_src[e][k]).then_inc(w2_in[e], 16)

            def body(b, par, first, last):
                if routes(b):
                    store_x1(b - 2, par)
                    store_x1T(b - 2, par)

            def store_x1(c, par):
                sp.wait_ge(x1_done, c + 1)
                sp.dma_start(x1_dram[bass.ds(c, 1)].rearrange("a (t p) d -> p (a t) d", p=P), x1[:, par])\
                    .then_inc(x1_out[par], 16)

            def store_x1T(c, par):
                sp.wait_ge(x1T_read, c + 1)
                sp.dma_start(x1T_dram[bass.ds(c, 1)].rearrange("a p s n -> p (a s) n"), x1T[:, par])\
                    .then_inc(x1T_out[par], 16)
            over_batches(sp, body)
            for c in (NB - 2, NB - 1):
                store_x1(c, c % 2)
                store_x1T(c, c % 2)
            for par in range(2):
                sp.wait_ge(x1T_out[par], 16 * NB // 2 + 16)
            for par in range(2):
                sp.wait_ge(x1_out[par], 16 * NB // 2 + 16)

        @block.gpsimd
        def _(pool):
            steps = [0]

            def then_wait(ins):
                steps[0] += 1
                ins.then_inc(pool_step, 1)
                pool.wait_ge(pool_step, steps[0])
            pool.memset(ident[:, :], 0.0).then_inc(pool_step, 1)
            pool.memset(ident16[:, :], 0.0).then_inc(pool_step, 1)
            pool.wait_ge(pool_step, 2)
            for m in (ident, ident16):
                pool.affine_select(out=m[:, :], in_=m[:, :], compare_op=ALU.not_equal, fill=1.0, base=0,
                                   pattern=[[-1, P]], channel_multiplier=1).then_inc(consts, 1)
            pool.memset(minus_half[:, :], -0.5).then_inc(consts, 1)
            pool.memset(xT[:, 0:1], 0.0).then_inc(consts, 1)
            pool.memset(feat[:, :, :], 0.0).then_inc(consts, 1)
            pool.memset(v_aug[:, :, :, :, :], 0.0).then_inc(pool_step, 1)
            pool.wait_ge(pool_step, 3)
            for par in range(2):
                pool.memset(v_aug[:, par, :, :, DH:DH + 1].rearrange("p t h o -> p (t h) o"), 1.0)\
                    .then_inc(consts, 1)
            pool.iota(iota_i[:, :, :], pattern=[[0, NT], [1, NE]], base=-100, channel_multiplier=0)\
                .then_inc(consts, 1)
            pool.iota(place_i[:, :, :], pattern=[[NTOK, 2], [P, NT]], base=0, channel_multiplier=1).then_inc(consts, 1)
            pool.memset(ones16[:, :], 1.0).then_inc(consts, 1)
            pool.wait_ge(consts, 10)
            pool.affine_select(out=tri[:, :], in_=ones16[:, :], compare_op=ALU.is_gt, fill=0.0, base=0,
                               pattern=[[1, P]], channel_multiplier=-1).then_inc(consts, 1)
            for e in range(NE):
                pool.memset(next_slot[:, e:e + 1], float(e * CAP)).then_inc(consts, 1)
            pool.memset(pad_rows[:, :, 0:P + 1], 0.0).then_inc(pad_done, 1)
            pool.memset(pad_rows[:, :, P + 1:P + 2].bitcast(I32), 2 * NTOK).then_inc(pad_done, 1)
            pool.wait_ge(pad_done, 2)
            for par in range(2):
                pool.dma_start(rows_dram[TAIL + par * P:TAIL + (par + 1) * P], pad_rows[:, par, :])\
                    .then_inc(rows_out[par], 16)

            def line_products(c):
                pool.wait_ge(pts_read, 2 * (c + 1))
                pool.wait_ge(prodB_read, c)
                for dst, many, one in products(prodB, 0, 1):
                    pool.tensor_tensor(dst, many, one, ALU.mult).then_inc(prodB_done, 1)

            def inv_std(c):
                pool.wait_ge(var_done, c + 1)
                pool.tensor_tensor(rstd[:, :], vareps[:, :], minus_half[:, :], ALU.pow).then_inc(rstd_done, 1)

            def mask(b, g, chunks=range(NCHUNK)):
                for c in chunks:
                    pool.wait_ge(s_exp, NCHUNK * HP * b + NCHUNK * g + c + 1)
                    pool.sem_inc(parted, 1)
                    for col, n, step in SQUARES[c]:
                        v = probs[:, g % 2, c, col:col + (n - 1) * step + P] if step == P or n == 1 else None
                        if v is None:
                            v = probs[:, g % 2, c, col:col + n * step].rearrange("p (n k) -> p n k", n=n)[:, :, 0:P]
                        else:
                            v = v.rearrange("p (n k) -> p n k", n=n)
                        pool.affine_select(out=v, in_=v, compare_op=ALU.is_ge, fill=0.0, base=0,
                                           pattern=[[0, n], [1, P]], channel_multiplier=-1).then_inc(masked, 1)
            line_products(0)

            def body(b, par, first, last):
                if routes(b):
                    inv_std(b - 2)
                mask(b, 0, (0, 1))
                if not last:
                    line_products(b + 1)
                mask(b, 0, (2, 3, 4))
                mask(b, 1, (0, 1, 2))
                for g, t in ((1, 0), (2, 1), (3, 3)):
                    if sends(b):
                        dispatch(pool, b - 3, 1 - par, (t,))
                    mask(b, g, (3, 4) if g == 1 else (0, 1, 2))
                    if g == 2:
                        if sends(b):
                            dispatch(pool, b - 3, 1 - par, (2,))
                        mask(b, 2, (3, 4))
                mask(b, 3, (3, 4))
            over_batches(pool, body)
            inv_std(NB - 2)
            dispatch(pool, NB - 3, 1, range(NT))
            inv_std(NB - 1)
        NMASK = sum(len(v) for v in SQUARES.values())
        NPROD = 6

        @block.tensor
        def _(pe):
            pe.wait_ge(consts, CONSTS)
            pe.wait_ge(wts_in, 16 * len(loads))
            for j in range(5):
                if j >= 2:
                    pe.wait_ge(wT_read, j - 1)
                pe.transpose(W[j % 2][:, 0:P], w_nat[:, j, :], ident[:, :]).then_inc(wT_full, 1)

            def transpose_x(c, par):
                pe.wait_ge(xin_in[par], 16 * (c // 2 + 1) if isinstance(c, int) else 16 * ((c - par) // 2 + 1))
                for t in range(NT):
                    mm = pe.transpose(W0[:, t * P:(t + 1) * P], x_in[:, par, t, :], ident[:, :])
                mm.then_inc(xT_full, 1)

            def project_points(c, half):
                w = W[(half + 1) % 2]
                if half == 0:
                    pe.wait_ge(xT_read, c + 1)
                for j in range(2):
                    t = 2 * half + j
                    pe.matmul(w[:, 2 * j * P:2 * (j + 1) * P], xT[:, 1 + t * P:1 + (t + 1) * P], w_allT[:, 0:2 * P],
                              start=True, stop=False, skip_group_check=True)
                    mm = pe.matmul(w[:, 2 * j * P:2 * (j + 1) * P].rearrange("p (a n) -> p a n", a=2)[:, :, 0:H * 4],
                                   xT[:, t * P:(t + 1) * P], w_prevT[:, :].rearrange("p (a n) -> p a n", a=2),
                                   start=False, stop=True, skip_group_check=True)
                mm.then_inc(pts_full, 1)

            def project_values(c):
                pe.wait_ge(pts_read, 2 * (c + 1))
                for t in range(NT):
                    mm = pe.matmul(W0[:, t * P:(t + 1) * P], xT[:, 1 + t * P:1 + (t + 1) * P], w_allT[:, 2 * P:3 * P],
                                   start=True, stop=True)
                mm.then_inc(val_full, 1)

            def transpose_feat(c, g):
                w = W[(g + 1) % 2][:, :].bitcast(FP16).rearrange("p (s n) -> p s n", s=2)
                if g == 0:
                    pe.wait_ge(feat_done, c + 1)
                elif g >= 2 or isinstance(c, int) and c == 0:
                    pe.wait_ge(featT_read, HP * c + g - 1)
                for s in range(2):
                    for t in range(NT):
                        first = s * NT * H + t * H + 4 * g
                        mm = pe.transpose(w[:, s, t * P:(t + 1) * P],
                                          feat[:, first:first + 4, :].rearrange("p h f -> p (h f)"), ident16[:, :])
                mm.then_inc(featT_full, 1)

            MATES = len(BANK_MATE)
            mates = [0]

            def scores(b, par, g, chunks):
                if chunks[0] == 0:
                    mates[0] = 0
                for c in chunks:
                    n = NCHUNK * HP * b + NCHUNK * g + c
                    if not (isinstance(n, int) and n < 2):
                        pe.wait_ge(s_exp, n - 1)
                    if c == 0:
                        pe.wait_ge(featT_read, HP * b + g + 1)
                    for (j, kb), (cc, col) in PIECES.items():
                        if cc == c:
                            q = qkT[32 * j:32 * j + 32, par, g, 0, kb * P:T]
                            k = qkT[32 * j:32 * j + 32, par, g, 1, kb * P:(kb + 1) * P]
                            if (j, kb) in BANK_MATE:
                                mates[0] += 1
                                pe.wait_ge(mate_done, MATES * (HP * b + g) + mates[0])
                            mm = pe.matmul(S[(g + c) % 2][:, col:col + T - kb * P], k, q, start=True, stop=True)
                            if (j, kb) in BANK_MATE.values():
                                mm.then_inc(mate_done, 1)
                    mm.then_inc(s_full, 1)

            def weigh(b, par, g, blocks):
                n = HP * b + g
                if blocks[0] == 0:
                    pe.wait_ge(masked, NMASK * (n + 1))
                    if not (isinstance(n, int) and n < 2):
                        pe.wait_ge(o_read, n - 1)
                for kb in blocks:
                    for j in range(4):
                        c, col = PIECES[(j, kb)]
                        mm = pe.matmul(O[g % 2][32 * j:32 * j + 32, kb * P:T], v_aug[:, par, kb, 4 * g + j, :],
                                       probs[:, g % 2, c, col:col + T - kb * P], start=(kb == 0), stop=(kb == NT - 1),
                                       skip_group_check=True)
                if blocks[-1] == NT - 1:
                    mm.then_inc(pv_done, 1)

            def transpose_out(c, t, after):
                if t == 0:
                    pe.wait_ge(o_read, HP * (c + 1))
                    pe.wait_ge(pts_read, 2 * (c + 3) if after else 2 * NB)
                    if not (isinstance(c, int) and c < 2):
                        pe.wait_ge(rank_read, c)
                elif t == 1:
                    if after:
                        pe.wait_ge(val_read, c + 3)
                    else:
                        pe.wait_ge(featT_read, HP * NB)
                        pe.wait_ge(y_read, c)
                elif t > 1:
                    pe.wait_ge(outT_read, NT * c + t - 1)
                for g in range(HP):
                    mm = pe.transpose(W[(t + 1) % 2][:, g * P:(g + 1) * P], oT_raw[:, g, t * P:(t + 1) * P], ident[:, :])
                mm.then_inc(outT_full, 1)

            def transpose_o(c):
                pe.wait_ge(outT_read, NT * (c + 1))
                for t in range(NT):
                    mm = pe.transpose(W0[:, t * P:(t + 1) * P], o_tok[:, t, :], ident[:, :])
                mm.then_inc(oT_full, 1)

            def project_out(c):
                pe.wait_ge(oT_read, c + 1)
                for t in range(NT):
                    mm = pe.matmul(W0[:, t * P:(t + 1) * P], oT[:, t * P:(t + 1) * P], w_oT[:, :], start=True, stop=True)
                mm.then_inc(y_full, 1)

            pe.wait_ge(wT_read, 5)
            pe.wait_ge(bv_spread, 1)
            pe.matmul(W1[:, 0:P], bv_cols[:, :], w_oT[:, :], start=True, stop=True).then_inc(wT_full, 1)
            pe.transpose(W0[:, 0:NE], wr_raw[:, :], ident[0:NE, 0:NE]).then_inc(wT_full, 1)
            pe.wait_ge(wT_read, 7)
            transpose_x(0, 0)
            project_points(0, 0)
            project_points(0, 1)
            project_values(0)
            pe.wait_ge(val_read, 1)
            for g in range(HP):
                transpose_feat(0, g)
            pe.wait_ge(featT_read, HP)
            transpose_x(1, 1)

            def transpose_x1(c, par):
                pe.wait_ge(split_done, c + 1)
                pe.wait_ge(rank_read, c + 1)
                if not (isinstance(c, int) and c == NB - 1):
                    pe.wait_ge(outT_read, NT * (c + 1) + 3)
                halves = xrow[:, par, :, 0, 0:P].bitcast(FP16)
                w = W1[:, :].bitcast(FP16).rearrange("p (s n) -> p s n", s=2)
                for s in range(2):
                    for t in range(NT):
                        mm = pe.transpose(w[:, s, t * P:(t + 1) * P], halves[:, t, s * P:(s + 1) * P], ident16[:, :])
                mm.then_inc(x1T_full, 1)

            def router(c, par):
                pe.wait_ge(x1T_read, c + 1)
                for t in range(NT):
                    for n, (a, w) in enumerate(((0, 0), (0, 1), (1, 0))):
                        mm = pe.matmul(W1[:, t * NE:(t + 1) * NE], x1T[:, par, a, t * P:(t + 1) * P], wr_T[:, w, :],
                                       start=(n == 0), stop=(n == 2))
                mm.then_inc(logit_full, 1)

            def ranks(c):
                pe.wait_ge(picks_done, c + 1)
                if not (isinstance(c, int) and c > NB - 5):
                    pe.wait_ge(pts_read, 2 * (c + 4) + 1)
                else:
                    pe.wait_ge(featT_read, HP * NB)
                    pe.wait_ge(logit_read, c + 1)
                pe.matmul(W1[:, 0:NT * NE], tri[:, :], picks[:, :, :].rearrange("p t e -> p (t e)"), start=True,
                          stop=False, skip_group_check=True)
                for t in range(NT):
                    n = NT - t
                    src = spread(picks[:, t:t + 1, :], 1, n)
                    mm = pe.matmul(W1[:, (t + 1) * NE:(NT + 1) * NE].rearrange("p (n e) -> p n e", n=n), ones16[:, :],
                                   src, start=False, stop=(t == NT - 1), skip_group_check=True)
                mm.then_inc(rank_full, 1)

            def body(b, par, first, last):
                def logits(g, c):
                    scores(b, par, g, (c,))

                logits(0, 0)
                if not last:
                    project_points(b + 1, 0)
                logits(0, 1)
                if not last:
                    project_points(b + 1, 1)
                logits(0, 2)
                if not first:
                    weigh(b - 1, 1 - par, 3, (0,))
                logits(0, 3)
                if not first:
                    weigh(b - 1, 1 - par, 3, (1, 2, 3))
                logits(0, 4)
                if sends(b):
                    ranks(b - 3)
                if not last:
                    project_values(b + 1)
                logits(1, 0)
                if not first:
                    transpose_out(b - 1, 0, not last)
                    transpose_out(b - 1, 1, not last)
                logits(1, 1)
                if not first:
                    transpose_out(b - 1, 2, not last)
                    transpose_out(b - 1, 3, not last)
                logits(1, 2)
                weigh(b, par, 0, (0,))
                logits(1, 3)
                weigh(b, par, 0, (1, 2, 3))
                logits(1, 4)
                if not first:
                    transpose_o(b - 1)
                logits(2, 0)
                if routes(b):
                    transpose_x1(b - 2, par)
                logits(2, 1)
                if not first:
                    project_out(b - 1)
                logits(2, 2)
                weigh(b, par, 1, (0,))
                logits(2, 3)
                weigh(b, par, 1, (1, 2, 3))
                logits(2, 4)
                if routes(b):
                    router(b - 2, par)
                logits(3, 0)
                if not last:
                    if first:
                        pe.wait_ge(val_read, 2)
                    if routes(b):
                        pe.wait_ge(logit_read, b - 1)
                    transpose_feat(b + 1, 0)
                logits(3, 1)
                if not last:
                    if not first:
                        pe.wait_ge(y_read, b)
                    transpose_feat(b + 1, 1)
                logits(3, 2)
                weigh(b, par, 2, (0,))
                if not last:
                    transpose_feat(b + 1, 2)
                logits(3, 3)
                weigh(b, par, 2, (1, 2, 3))
                if not last:
                    transpose_feat(b + 1, 3)
                logits(3, 4)
                if ahead(b):
                    pe.wait_ge(featT_read, HP * (b + 2))
                    transpose_x(b + 2, par)
            over_batches(pe, body)
            weigh(NB - 1, 1, 3, (0, 1, 2, 3))
            ranks(NB - 3)
            for t in range(NT):
                transpose_out(NB - 1, t, False)
            transpose_x1(NB - 2, 0)
            transpose_o(NB - 1)
            router(NB - 2, 0)
            project_out(NB - 1)
            ranks(NB - 2)
            transpose_x1(NB - 1, 1)
            router(NB - 1, 1)
            ranks(NB - 1)

        @block.scalar
        def _(act):
            def copy_points(c, half):
                act.wait_ge(pts_full, 2 * c + half + 1)
                if half == 0:
                    act.wait_ge(prodB_done, NPROD * c)
                    act.wait_ge(prodB_read, c)
                act.copy(p12[:, :, :, 2 * half:2 * half + 2].rearrange("p a s t h c -> p (a s) t (h c)"),
                         W[(half + 1) % 2][:, :].rearrange("p (t a n) -> p a t n", t=2, a=4)).then_inc(pts_read, 1)

            def copy_values(c, par):
                act.wait_ge(val_full, c + 1)
                act.copy(v_aug[:, par, :, :, 0:DH].rearrange("p t h d -> p (t h) d"),
                         W0[:, :].rearrange("p (n d) -> p n d", d=DH)).then_inc(val_read, 1)

            def exps(b, g, chunks):
                for c in chunks:
                    n = HP * b + g
                    act.wait_ge(s_full, NCHUNK * n + c + 1)
                    if c == 0 and not (isinstance(n, int) and n < 2):
                        act.wait_ge(pv_done, n - 1)
                    act.activation(probs[:, g % 2, c, :], S[(g + c) % 2][:, :], ACT.Exp,
                                   scale=-SCALE / SPLIT_UP ** 2).then_inc(s_exp, 1)

            def copy_out(b, g):
                act.wait_ge(pv_done, HP * b + g + 1)
                if g == 0:
                    act.wait_ge(outT_full, NT * b)
                act.copy(oT_raw[:, g, :], O[g % 2][:, :]).then_inc(o_read, 1)

            def copy_oT(c):
                act.wait_ge(oT_full, c + 1)
                act.copy(oT[:, :], W0[:, :]).then_inc(oT_read, 1)

            def copy_x1T(c, par):
                act.wait_ge(x1T_full, c + 1)
                act.wait_ge(x1T_out[par], 16 * ((c - par) // 2) + 16)
                act.copy(x1T[:, par].rearrange("p s n -> p (s n)"), W1[:, :].bitcast(FP16)).then_inc(x1T_read, 1)

            def tanh_logits(c):
                act.wait_ge(logit_read, c + 1)
                act.activation(rt["prob"][:, :, :], rt["logit"][:, :, :], ACT.Tanh, scale=0.5).then_inc(tanh_done, 1)

            def load_x(c, par):
                act.wait_ge(xres_done, c - 1) if not (isinstance(c, int) and c < 2) else None
                act.dma_start(x_in[:, par], x[bass.ds(c, 1)].rearrange("a (t p) d -> p (a t) d", p=P))\
                    .then_inc(xin_in[par], 16)

            load_x(0, 0)
            load_x(1, 1)
            copy_points(0, 0)
            copy_points(0, 1)
            copy_values(0, 0)

            def body(b, par, first, last):
                if ahead(b):
                    load_x(b + 2, par)
                exps(b, 0, (0,))
                if not last:
                    copy_points(b + 1, 0)
                exps(b, 0, (1,))
                if not last:
                    copy_points(b + 1, 1)
                exps(b, 0, (2, 3))
                if not first:
                    copy_out(b - 1, 3)
                exps(b, 0, (4,))
                if not last:
                    copy_values(b + 1, 1 - par)
                exps(b, 1, (0, 1, 2, 3))
                copy_out(b, 0)
                exps(b, 1, (4,))
                if not first:
                    copy_oT(b - 1)
                exps(b, 2, (0,))
                if routes(b):
                    copy_x1T(b - 2, par)
                exps(b, 2, (1, 2, 3))
                copy_out(b, 1)
                exps(b, 2, (4,))
                exps(b, 3, (0, 1))
                if routes(b):
                    tanh_logits(b - 2)
                exps(b, 3, (2, 3))
                copy_out(b, 2)
                exps(b, 3, (4,))
            over_batches(act, body)
            copy_out(NB - 1, 3)
            copy_x1T(NB - 2, 0)
            copy_oT(NB - 1)
            tanh_logits(NB - 2)
            copy_x1T(NB - 1, 1)
            tanh_logits(NB - 1)

        @block.vector
        def _(dve):
            base, count = [0], [0]

            def chain(ins):
                ins.then_inc(dve_step, 1)
                count[0] += 1
                dve.wait_ge(dve_step, base[0] + count[0])

            dve.wait_ge(consts, CONSTS)
            for j in range(5):
                dve.wait_ge(wT_full, j + 1)
                src = W[j % 2][:, 0:P]
                if j == 2:
                    ins = dve.tensor_copy(w_allT[:, 2 * P:3 * P], src)
                elif j == 4:
                    ins = dve.tensor_copy(w_oT[:, :], src)
                else:
                    src = src.rearrange("p (s h c) -> p s h c", s=2, c=4)
                    dst = (w_allT[:, j * P:(j + 1) * P] if j < 2 else w_prevT[:, :])\
                        .rearrange("p (s h c) -> p s h c", s=2, c=4)
                    for c in range(4):
                        for s in range(2):
                            is_k = j < 2 and s == 1
                            ins = dve.tensor_scalar(dst[:, s, :, 3 - c if is_k else c], src[:, s, :, c],
                                                    -1.0 if c == (3 if is_k else 1) else 1.0, None, ALU.mult)
                ins.then_inc(wT_read, 1)
            dve.wait_ge(wts_in, 16 * len(loads))
            dve.tensor_copy(bv_cols[:, :], spread(bv_col[:, :], 1, P)).then_inc(bv_spread, 1)
            dve.wait_ge(wT_full, 6)
            dve.tensor_tensor(bo_bc[:, :], W1[:, 0:P], bo_bc[:, :], ALU.add).then_inc(wT_read, 1)
            dve.wait_ge(wT_full, 7)
            dve.tensor_scalar(wr_T[:, 0, :], W0[:, 0:NE], UP, None, ALU.mult).then_inc(rank_read, 1)
            dve.wait_ge(rank_read, 1)
            dve.scalar_tensor_tensor(out=wr_T[:, 1, :], in0=W0[:, 0:NE], scalar=UP, in1=wr_T[:, 0, :], op0=ALU.mult,
                                     op1=ALU.subtract).then_inc(wT_read, 1)
            dve.tensor_copy(iota_e[:, :, :], iota_i[:, :, :])
            dve.tensor_copy(rb4[:, :, :], spread(rb_bc[:, :].rearrange("p (o e) -> p o e", o=1), 1, NT))
            dve.wait_ge(wT_read, 7)

            def copy_xT(c):
                dve.wait_ge(xT_full, c + 1)
                dve.wait_ge(val_full, c)
                dve.tensor_copy(xT[:, 1:T + 1], W0[:, :]).then_inc(xT_read, 1)

            def line_terms(c):
                dve.wait_ge(pts_read, 2 * (c + 1))
                for dst, many, one in products(prodA, 1, 0):
                    ins = dve.tensor_tensor(dst, many, one, ALU.mult)
                chain(ins)

            def subtract_terms(c):
                dve.wait_ge(prodB_done, NPROD * (c + 1))
                chain(dve.tensor_tensor(prodA[:, :, :], prodA[:, :, :], prodB[:, :, :], ALU.subtract))

            def square_lines():
                chain(dve.tensor_tensor(prodB[:, :, :], prodA[:, :, :], prodA[:, :, :], ALU.mult))

            def sum_squares():
                chain(dve.tensor_reduce(nrm[:, :], prodB[:, :, :], AX.X, ALU.add))

            def inverse_norms():
                chain(dve.tensor_scalar(nrm[:, :], nrm[:, :], 1e-24, None, ALU.max))
                dve.tensor_scalar(nhalf[:, :], nrm[:, :], -0.5, None, ALU.mult)
                chain(dve.tensor_scalar(rs_b[:, :].bitcast(I32), nrm[:, :].bitcast(I32), 1, None,
                                        ALU.logical_shift_right))
                chain(dve.tensor_scalar(rs_a[:, :].bitcast(I32), rs_b[:, :].bitcast(I32), -1.0, float(0x5f3759df),
                                        ALU.mult, ALU.add))
                for _ in range(3):
                    chain(dve.tensor_tensor(rs_b[:, :], rs_a[:, :], rs_a[:, :], ALU.mult))
                    chain(dve.tensor_tensor(rs_b[:, :], rs_b[:, :], nhalf[:, :], ALU.mult))
                    chain(dve.scalar_tensor_tensor(out=rs_a[:, :], in0=rs_b[:, :], scalar=1.5, in1=rs_a[:, :],
                                                   op0=ALU.add, op1=ALU.mult))

            def write_features(c):
                rs = spread(rs_a[:, :].rearrange("p (h o) -> p h o", o=1), 2, LINE)
                chain(dve.scalar_tensor_tensor(out=prodB[:, :, :], in0=prodA[:, :, :], scalar=SPLIT_UP, in1=rs,
                                               op0=ALU.mult, op1=ALU.mult))
                dve.wait_ge(featT_full, HP * c)
                chain(dve.tensor_copy(feat[:, :, 0:LINE], prodB[:, :, :]))
                dve.tensor_tensor(feat[:, :, LINE:2 * LINE], prodB[:, :, :], feat[:, :, 0:LINE], ALU.subtract)\
                    .then_inc(prodB_read, 1)
                dve.wait_ge(prodB_read, c + 1)
                f = feat[:, :, :].rearrange("p (s h) l -> p s h l", s=2)
                dve.tensor_copy(f[:, 0, :, 2 * LINE:4 * LINE], f[:, 0, :, 0:2 * LINE])
                dve.tensor_copy(f[:, 1, :, 2 * LINE:3 * LINE], f[:, 1, :, LINE:2 * LINE])
                dve.tensor_copy(f[:, 1, :, 3 * LINE:4 * LINE], f[:, 1, :, 0:LINE]).then_inc(feat_done, 1)

            def copy_feat(c, par, g):
                dve.wait_ge(featT_full, HP * c + g + 1)
                dve.tensor_copy(qkT[:, par, g, :, :].rearrange("p s n -> p (s n)"),
                                W[(g + 1) % 2][:, :].bitcast(FP16)).then_inc(featT_read, 1)

            def normalise(c, t):
                dve.wait_ge(outT_full, NT * c + t + 1)
                w = W[(t + 1) % 2][:, :].rearrange("p (h n) -> p h n", n=32)
                chain(dve.reciprocal(rden[:, t, :].rearrange("p (h o) -> p h o", o=1), w[:, :, DH:DH + 1]))
                dve.tensor_tensor(o_tok[:, t, :].rearrange("p (h d) -> p h d", d=DH), w[:, :, 0:DH],
                                  spread(rden[:, t, :].rearrange("p (h o) -> p h o", o=1), 2, DH), ALU.mult)\
                    .then_inc(outT_read, 1)

            def residual(c, par):
                dve.wait_ge(y_full, c + 1)
                dve.wait_ge(xres_done, c + 1)
                dve.tensor_tensor(ysum[:, :, :], W0[:, :].rearrange("p (t n) -> p t n", t=NT), xres[:, par, :, :],
                                  ALU.add).then_inc(y_read, 1)
                dve.wait_ge(y_read, c + 1)
                for t in range(NT):
                    ins = dve.bn_stats(stats[:, t, :], ysum[:, t, :])
                chain(ins)
                dve.sem_inc(parted, 1)
                for t in range(NT):
                    ins = dve.bn_aggr(meanvar[:, t, :], stats[:, t, :])
                chain(ins)
                dve.tensor_scalar(vareps[:, :], meanvar[:, :, 1], EPS, None, ALU.add).then_inc(var_done, 1)

            def norm_out(c, par):
                dve.wait_ge(rstd_done, c + 1)
                dve.wait_ge(x1_out[par], 16 * ((c - par) // 2) + 16)
                for t in range(NT):
                    ins = dve.tensor_scalar(x1[:, par, t, :], ysum[:, t, :], meanvar[:, t, 0:1], rstd[:, t:t + 1],
                                            ALU.subtract, ALU.mult)
                ins.then_inc(x1_done, 1)

            def split(c, par):
                dve.wait_ge(x1_done, c + 1)
                dve.wait_ge(rows_out[par], 2 * NT * 16 * ((c - par) // 2) + 16)
                h = xrow[:, par, :, 0, 0:P].bitcast(FP16)
                chain(dve.tensor_scalar(h[:, :, 0:P], x1[:, par, :, :], UP, None, ALU.mult))
                chain(dve.scalar_tensor_tensor(out=h[:, :, P:2 * P], in0=x1[:, par, :, :], scalar=UP,
                                               in1=h[:, :, 0:P], op0=ALU.mult, op1=ALU.subtract))
                dve.tensor_copy(xrow[:, par, :, 1, 0:P], xrow[:, par, :, 0, 0:P]).then_inc(split_done, 1)

            def read_logits(c):
                dve.wait_ge(logit_full, c + 1)
                dve.scalar_tensor_tensor(out=rt["logit"][:, :, :], in0=W1[:, 0:NT * NE].rearrange("p (t e) -> p t e", t=NT),
                                         scalar=1.0 / UP ** 2, in1=rb4[:, :, :], op0=ALU.mult, op1=ALU.add)\
                    .then_inc(logit_read, 1)

            def choose(c, par):
                dve.wait_ge(tanh_done, c + 1)
                prob, eq, cand, rest = (rt[n][:, :, :] for n in ("prob", "eq", "cand", "rest"))
                chain(dve.tensor_scalar(prob, prob, 0.5, 0.5, ALU.mult, ALU.add))
                for k, src in enumerate((prob, rest)):
                    if k:
                        chain(dve.scalar_tensor_tensor(out=rest, in0=one[:, 0], scalar=-4.0, in1=prob, op0=ALU.mult,
                                                       op1=ALU.add))
                    chain(dve.tensor_reduce(rmax[:, k, :], src, AX.X, ALU.max))
                    chain(dve.tensor_tensor(eq, src, per_expert(rmax[:, k, :]), ALU.is_equal))
                    chain(dve.tensor_tensor(cand, eq, iota_e[:, :, :], ALU.mult))
                    chain(dve.tensor_reduce(rmin[:, :], cand, AX.X, ALU.min))
                    chain(dve.tensor_tensor(one[:, k], cand, per_expert(rmin[:, :]), ALU.is_equal))
                dve.tensor_tensor(picks[:, :, :], one[:, 0], one[:, 1], ALU.add).then_inc(picks_done, 1)
                tail = xrow[:, par].rearrange("p t k w -> p k t w")
                dve.tensor_scalar(tail[:, :, :, P], rmax[:, :, :], 1.0 / (UP * H_UP), None, ALU.mult)
                chain(dve.tensor_copy(tail[:, :, :, P + 1].bitcast(I32), place_i[:, :, :]))
                dve.tensor_scalar(place_i[:, :, :], place_i[:, :, :], T, None, ALU.add)

            def per_expert(v):
                return spread(v.rearrange("p (t o) -> p t o", o=1), 2, NE)

            def slots(c, par):
                dve.wait_ge(rank_full, c + 1)
                slot = rt["slot"][:, :, :]
                chain(dve.tensor_tensor(slot, W1[:, 0:NT * NE].rearrange("p (t e) -> p t e", t=NT),
                                        spread(next_slot[:, :].rearrange("p (o e) -> p o e", o=1), 1, NT), ALU.add))
                dve.tensor_tensor(next_slot[:, :], next_slot[:, :], W1[:, NT * NE:(NT + 1) * NE], ALU.add)\
                    .then_inc(rank_read, 1)
                for k in range(2):
                    ins = dve.tensor_tensor(oneslot[:, k], one[:, k], slot, ALU.mult)
                chain(ins)
                chain(dve.tensor_reduce(slot_f[:, :, :], oneslot[:, :, :, :], AX.X, ALU.add))
                dve.tensor_copy(slot_i[:, par], slot_f[:, :, :]).then_inc(rows_ready, 1)

            def add_bias(c, par):
                dve.wait_ge(xT_full, c + 1)
                dve.tensor_tensor(xres[:, par, :, :], x_in[:, par, :, :],
                                  spread(bo_bc[:, :].rearrange("p (o n) -> p o n", o=1), 1, NT), ALU.add)\
                    .then_inc(xres_done, 1)

            copy_xT(0)
            line_terms(0)
            subtract_terms(0)
            square_lines()
            sum_squares()
            inverse_norms()
            write_features(0)
            for g in range(HP):
                copy_feat(0, 0, g)
            copy_xT(1)
            add_bias(0, 0)

            def body(b, par, first, last):
                count[0] = 0
                if sends(b):
                    choose(b - 3, 1 - par)
                if not last:
                    line_terms(b + 1)
                if sends(b):
                    slots(b - 3, 1 - par)
                if not last:
                    subtract_terms(b + 1)
                if not first:
                    normalise(b - 1, 0)
                    normalise(b - 1, 1)
                if not last:
                    square_lines()
                if not first:
                    normalise(b - 1, 2)
                    normalise(b - 1, 3)
                if not last:
                    sum_squares()
                if routes(b):
                    norm_out(b - 2, par)
                    split(b - 2, par)
                if not last:
                    inverse_norms()
                    write_features(b + 1)
                if routes(b):
                    read_logits(b - 2)
                if not first:
                    residual(b - 1, 1 - par)
                if not last:
                    for g in range(HP):
                        copy_feat(b + 1, 1 - par, g)
                if ahead(b):
                    copy_xT(b + 2)
                if not last:
                    add_bias(b + 1, 1 - par)
                base[0] = base[0] + count[0]
            per = 4 + (4 + 12 + 2) + 2 + 2 + 13 + 3
            base[0] = count[0]
            body(0, 0, True, False)
            for b in range(1, PEEL):
                body(b, b % 2, False, False)
            start = base[0]
            with dve.Fori(PEEL // 2, NB // 2 - 1) as i:
                base[0] = start + (i - PEEL // 2) * (2 * per)
                body(2 * i, 0, False, False)
                assert count[0] == per, count[0]
                body(2 * i + 1, 1, False, False)
                assert count[0] == per
            base[0] = start + (NB // 2 - 1 - PEEL // 2) * 2 * per
            body(NB - 2, 0, False, False)
            body(NB - 1, 1, False, True)
            count[0] = 0
            choose(NB - 3, 1)
            slots(NB - 3, 1)
            norm_out(NB - 2, 0)
            split(NB - 2, 0)
            for t in range(NT):
                normalise(NB - 1, t)
            residual(NB - 1, 1)
            read_logits(NB - 2)
            choose(NB - 2, 0)
            norm_out(NB - 1, 1)
            split(NB - 1, 1)
            slots(NB - 2, 0)
            read_logits(NB - 1)
            choose(NB - 1, 1)
            slots(NB - 1, 1)

        block_scope.close()
        phase1.close()

        NSH = NTOK // UNIT
        NRT = 2 * NTOK // UNIT + NE
        NRING = 8
        ZRING = 4
        phase2 = ctx.enter_context(ExitStack())

        def sb2(name, shape, dt=FP32):
            return phase2.enter_context(nc.sbuf_tensor(name, shape, dt))

        w_T = sb2("w_T", [P, NX, 2, 6, P], FP16)
        sch = {n: sb2("sch_" + n, [P, NE]) for n in ("count", "units", "end", "gap")}
        sch_i = sb2("sch_i", [P, NE], I32)
        slot_end = sb2("slot_end", [P, NE], I32)
        unit_i = sb2("unit_i", [P, NRT], I32)
        unit_f = sb2("unit_f", [P, NRT])
        past = sb2("past", [P, 2, NE, NRT])
        turn_f = sb2("turn_f", [P, NRT // NRING])
        turn_experts = sb2("turn_experts", [P, NRT // NRING], I32)
        unit_row = sb2("unit_row", [P, NRT], I32)
        x1_in = sb2("x1_in", [P, NRING, 2, P])
        rows = sb2("rows", [P, NRING, 2, ROW])
        xT_sh = sb2("xT_sh", [P, NRING, 2, UNIT], FP16)
        xT_rt = sb2("xT_rt", [P, 2, 2, UNIT], FP16)
        th = sb2("th", [P, 2, 2 * UNIT])
        gated = sb2("gated", [P, 2, 2 * UNIT])
        hid = sb2("hid", [P, 2, 2 * UNIT])
        hid16 = sb2("hid16", [P, 2, 2, 2 * UNIT], FP16)
        y = sb2("y", [P, NRING, 2, P])
        acc = sb2("acc", [P, NTOK // P, P])
        z = sb2("z", [P, ZRING, 2, NT, P])
        stats2 = sb2("stats2", [P, 2, NT, 6])
        meanvar2 = sb2("meanvar2", [P, ZRING, NT, 2])
        vareps2 = sb2("vareps2", [P, ZRING, NT])
        rstd2 = sb2("rstd2", [P, ZRING, NT])
        shift2 = sb2("shift2", [P, ZRING, NT])
        res = sb2("res", [P, 2, NT, P])

        w2T_full = sem("w2T_full"); w2T_hi = sem("w2T_hi"); w2T_lo = sem("w2T_lo")
        consts2 = sem("consts2"); units_done = sem("units_done"); slot_end_done = sem("slot_end_done"); table_done = sem("table_done")
        pads_out = sem("pads_out")
        sh_in = [sem(f"sh_in{r}") for r in range(NRING)]
        rt_in = [sem(f"rt_in{r}") for r in range(NRING)]
        xT2_full = sem("xT2_full"); xT2_read = sem("xT2_read")
        gu_full = sem("gu_full"); gate_tanh = sem("gate_tanh"); hid_done = sem("hid_done"); hi_done = sem("hi_done")
        lo_done = sem("lo_done"); down_full = sem("down_full"); acc_done = sem("acc_done")
        y_ready = sem("y_ready"); z_out = [sem(f"z_out{r}") for r in range(NRING)]
        z_in = [sem(f"z_in{r}") for r in range(ZRING)]; zsum_done = sem("zsum_done"); tot_done = sem("tot_done")
        stats2_done = sem("stats2_done"); aggr_done = sem("aggr_done")
        var2_done = sem("var2_done"); rstd2_done = sem("rstd2_done"); shift_done = sem("shift_done")
        res_done = sem("res_done"); res_out = [sem("res_out0"), sem("res_out1")]
        step2 = sem("step2"); stats_step = sem("stats_step"); gated_done = sem("gated_done")
        SHARED = NE

        def place(e):
            return (e - 1) % NX

        def over_units(eng, body):
            R = NRING
            for u in range(R):
                body(u, u, u, 0, True)
            with eng.Fori(1, NSH // R) as i:
                for r in range(R):
                    body(R * i + r, R * i + r, r, i, True)
            for u in range(R):
                body(NSH + u, u, u, 0, False)
            with eng.Fori(1, NRT // R - 1) as i:
                for r in range(R):
                    body(NSH + R * i + r, R * i + r, r, i, False)
            for r in range(R):
                body(NSH + NRT - R + r, NRT - R + r, r, NRT // R - 1, False)
        assert NSH % NRING == 0 and NRT % NRING == 0

        def over_results(eng, body, after):
            for b in range(ZRING):
                body(b, b, 0)
            with eng.Fori(1, NB // ZRING) as i:
                for r in range(ZRING):
                    body(ZRING * i + r, r, i)
            for b in range(NB, NB + after):
                body(b, b % ZRING, b // ZRING)

        RES_AHEAD = 2

        def there(b):
            return not isinstance(b, int) or 0 <= b < NB
        assert NB % ZRING == 0

        block2 = ctx.enter_context(nc.Block())

        @block2.sync
        def _(sp):
            def body(u, n, r, i, shared):
                if shared:
                    if not isinstance(i, int):
                        sp.wait_ge(acc_done, n - NRING + 1)
                    half = r % 2
                    b = (n - half) // 2
                    sp.dma_start(xT_sh[:, r], x1T_dram[bass.ds(b, 1), :, :, half * UNIT:(half + 1) * UNIT]
                                 .rearrange("a p s n -> p (a s) n")).then_inc(sh_in[r], 16)
                    sp.dma_start(x1_in[:, r], x1_dram[bass.ds(b, 1), half * UNIT:(half + 1) * UNIT, :]
                                 .rearrange("o (a p) d -> p (o a) d", p=P)).then_inc(sh_in[r], 16)
                    return
                if isinstance(u, int) and u == NSH:
                    for par in range(2):
                        sp.wait_ge(rows_out[par], 2 * NT * 16 * NB // 2 + 16)
                    sp.wait_ge(slot_end_done, 1)
                    for e in range(NE):
                        at = sp.value_load(slot_end[0:1, e:e + 1], min_val=e * CAP, max_val=e * CAP + NTOK)
                        sp.dma_start(rows_dram[bass.ds(at, UNIT)].rearrange("(a p) w -> p a w", p=P), pad_rows[:, :, :])\
                            .then_inc(pads_out, 16)
                    sp.wait_ge(pads_out, 16 * NE)
                    sp.wait_ge(table_done, 1)
                if not (isinstance(i, int) and i == 0):
                    sp.wait_ge(z_out[r], 2 * 16 * i)
                at = sp.value_load(unit_row[0:1, bass.ds(n, 1)], min_val=0, max_val=TAIL)
                sp.dma_start(rows[:, r], rows_dram[bass.ds(at, UNIT)].rearrange("(a p) w -> p a w", p=P))\
                    .then_inc(rt_in[r], 16)
            over_units(sp, body)
            for r in range(NRING):
                sp.wait_ge(z_out[r], 2 * 16 * (NRT // NRING))

            def load_z(b, r):
                for k in range(2):
                    sp.dma_start(z[:, r, k], z_dram[bass.ds(b * T + k * NTOK, T)].rearrange("(t p) d -> p t d", p=P))\
                        .then_inc(z_in[r], 16)
            for b in range(ZRING):
                load_z(b, b)

            def finish(b, r, more):
                if more:
                    sp.wait_ge(tot_done, b + 1)
                    load_z(b + ZRING, r)
                sp.wait_ge(res_done, RES_AHEAD + b + 1)
                sp.dma_start(out[bass.ds(b, 1)].rearrange("a (t p) d -> p (a t) d", p=P), res[:, r % 2])\
                    .then_inc(res_out[r % 2], 16)
            with sp.Fori(0, NB // ZRING - 1) as i:
                for r in range(ZRING):
                    finish(ZRING * i + r, r, True)
            for r in range(ZRING):
                finish(NB - ZRING + r, r, False)
            for par in range(2):
                sp.wait_ge(res_out[par], 16 * NB // 2)

        @block2.gpsimd
        def _(pool):
            pool.iota(unit_i[:, :], pattern=[[1, NRT]], base=0, channel_multiplier=0).then_inc(consts2, 1)
            count = [0]

            def chain(ins):
                ins.then_inc(step2, 1)
                count[0] += 1
                pool.wait_ge(step2, count[0])

            dispatch(pool, NB - 2, 0, range(NT))
            dispatch(pool, NB - 1, 1, range(NT))

            pool.wait_ge(consts2, 1)
            pool.tensor_copy(slot_end[:, :], next_slot[:, :]).then_inc(slot_end_done, 1)
            pool.tensor_copy(unit_f[:, :], unit_i[:, :])
            pool.wait_ge(units_done, 1)
            U, E, G = (sch[n][:, :] for n in ("units", "end", "gap"))
            pool.tensor_scalar(G, U, -float(UNIT), float(CAP), ALU.mult, ALU.add)
            chain(pool.tensor_copy(E[:, 0:1], U[:, 0:1]))
            for e in range(1, NE):
                chain(pool.tensor_tensor(E[:, e:e + 1], E[:, e - 1:e], U[:, e:e + 1], ALU.add))
            for e in range(NE):
                pool.tensor_scalar(past[:, 0, e, :], unit_f[:, :], E[:, e:e + 1], None, ALU.is_ge)
                ins = pool.tensor_scalar(past[:, 1, e, :], unit_f[:, :], E[:, e:e + 1], G[:, e:e + 1], ALU.is_ge, ALU.mult)
            chain(ins)
            n = NE
            while n > 1:
                n //= 2
                for k in range(2):
                    ins = pool.tensor_tensor(past[:, k, 0:n], past[:, k, 0:n], past[:, k, n:2 * n], ALU.add)
                chain(ins)
            chain(pool.tensor_scalar(past[:, 0, 0], past[:, 0, 0], float(NE - 1), None, ALU.min))
            turns = past[:, 0, 0].rearrange("p (i r) -> p i r", r=NRING)
            chain(pool.tensor_copy(turn_f[:, :], turns[:, :, NRING - 1]))
            for r in range(NRING - 2, -1, -1):
                chain(pool.tensor_scalar(turn_f[:, :], turn_f[:, :], float(NE), None, ALU.mult))
                chain(pool.tensor_tensor(turn_f[:, :], turn_f[:, :], turns[:, :, r], ALU.add))
            pool.tensor_copy(turn_experts[:, :], turn_f[:, :])
            chain(pool.tensor_scalar(unit_f[:, :], unit_f[:, :], float(UNIT), None, ALU.mult))
            chain(pool.tensor_tensor(unit_f[:, :], unit_f[:, :], past[:, 1, 0], ALU.add))
            pool.tensor_scalar(unit_row[:, :], unit_f[:, :], float(TAIL), None, ALU.min).then_inc(table_done, 1)

            def body(u, n, r, i, shared):
                if shared:
                    return
                pool.wait_ge(y_ready, n + 1)
                pool.sem_inc(parted, 1)
                for a in range(2):
                    pool.indirect_dma_start(
                        out=z_dram, in_=y[:, r, a, :], in_offset=None,
                        out_offset=bass.IndirectOffsetOnAxis(ap=rows[:, r, a, P + 1:P + 2].bitcast(I32), axis=0),
                        bounds_check=2 * NTOK - 1, oob_is_err=False).then_inc(z_out[r], 16)
            over_units(pool, body)

            def finish(b, r, i):
                if there(b):
                    pool.wait_ge(z_in[r], 32 * (i + 1))
                    pool.tensor_tensor(z[:, r, 0], z[:, r, 0], z[:, r, 1], ALU.add).then_inc(zsum_done, 1)
                if there(b - 2):
                    c = (r - 2) % ZRING
                    pool.wait_ge(var2_done, b - 1)
                    if not (isinstance(b, int) and b < ZRING):
                        pool.wait_ge(res_done, RES_AHEAD + b - 5)
                    pool.tensor_tensor(rstd2[:, c, :], vareps2[:, c, :], minus_half[:, :], ALU.pow)\
                        .then_inc(rstd2_done, 1)
            over_results(pool, finish, 2)

        @block2.tensor
        def _(pe):
            def transpose_weights(e):
                pe.wait_ge(w2_in[e], 48)
                for h, (a, n) in enumerate(((0, 4), (4, 2))):
                    if e:
                        pe.wait_ge(w2T_lo, 2 * e + h - 1)
                    for k in range(n):
                        mm = pe.transpose(W[h][:, k * P:(k + 1) * P], w_raw[:, e, a + k, :], ident[:, :])
                    mm.then_inc(w2T_full, 1)

            def gate_up(u, r, xT, e):
                if not (isinstance(u, int) and u < 2):
                    pe.wait_ge(hid_done, u - 1)
                for k in range(4):
                    for n, (a, w) in enumerate(((0, 0), (1, 0), (0, 1))):
                        mm = pe.matmul(S[r % 2][:, k * UNIT:(k + 1) * UNIT], weights(e, w, k), xT[:, a, :],
                                       start=(n == 0), stop=(n == 2))
                mm.then_inc(gu_full, 1)

            def weights(e, w, k):
                if isinstance(e, int):
                    return w_T[:, e, w, k, :]
                return w_T[:, bass.ds(e, 1), w, k, :].rearrange("p o n -> p (o n)")

            def down(u, r, e):
                pe.wait_ge(lo_done, u + 1)
                if isinstance(e, int) or isinstance(u, int) and u < NSH + 2:
                    if not (isinstance(u, int) and u < 2):
                        pe.wait_ge(acc_done, u - 1)
                else:
                    pe.wait_ge(y_ready, u - NSH - 1)
                par = r % 2
                for a in range(2):
                    n = 0
                    for k in range(2):
                        for h, w in ((0, 0), (0, 1), (1, 0)):
                            mm = pe.matmul(O[par][:, a * P:(a + 1) * P],
                                           hid16[:, par, h, k * UNIT + a * P:k * UNIT + (a + 1) * P],
                                           weights(e, w, 4 + k), start=(n == 0), stop=(n == 5))
                            n += 1
                mm.then_inc(down_full, 1)

            def transposes(n, r, i):
                pe.wait_ge(rt_in[r], 16 * (i + 1))
                if not (isinstance(n, int) and n < 2):
                    pe.wait_ge(xT2_read, n - 1)
                w = W[r % 2][:, 0:UNIT].bitcast(FP16).rearrange("p (s m) -> p s m", s=2)
                for s in range(2):
                    for a in range(2):
                        src = rows[:, r, a, s * P // 2:(s + 1) * P // 2].bitcast(FP16)
                        mm = pe.transpose(w[:, s, a * P:(a + 1) * P], src, ident16[:, :])
                mm.then_inc(xT2_full, 1)

            def experts_of(turn):
                return pe.value_load(turn_experts[0:1, bass.ds(turn, 1)], min_val=0, max_val=NE ** NRING - 1)

            def expert_of(experts, r):
                return (experts >> (NE.bit_length() - 1) * r) & NE - 1

            def body(u, n, r, i, shared):
                peeled = isinstance(n, int)
                if shared:
                    pe.wait_ge(sh_in[r], 32 * (i + 1))
                    gate_up(u, r, xT_sh[:, r], SHARED)
                    if not (peeled and n < 2):
                        down(u - 2, r - 2, SHARED)
                    if peeled:
                        transpose_weights(n + 1)
                    return
                if peeled and n == 0:
                    pe.wait_ge(table_done, 1)
                    pe.wait_ge(w2T_lo, 2 * NX)
                    transposes(0, 0, 0)
                if not (peeled and n == NRT - 1):
                    nxt = (r + 1) % NRING
                    transposes(n + 1, nxt, i if nxt else i + 1)
                if r == 0:
                    turn["now"] = experts_of(i)
                pe.wait_ge(xT2_read, n + 1)
                gate_up(u, r, xT_rt[:, r % 2], expert_of(turn["now"], r))
                if r >= 2:
                    down(u - 2, r - 2, expert_of(turn["now"], r - 2))
                elif peeled and n < 2:
                    down(u - 2, r - 2, SHARED)
                else:
                    if r == 0:
                        turn["before"] = experts_of(i - 1)
                    down(u - 2, r - 2, expert_of(turn["before"], NRING + r - 2))
            turn = {}
            transpose_weights(0)
            pe.wait_ge(w2T_lo, 2)
            over_units(pe, body)
            for r in (NRING - 2, NRING - 1):
                down(NSH + NRT - NRING + r, r, expert_of(turn["now"], r))

        @block2.scalar
        def _(act):
            def split_weights(e):
                for h, (a, n) in enumerate(((0, 4), (4, 2))):
                    act.wait_ge(w2T_full, 2 * e + h + 1)
                    act.activation(w_T[:, place(e), 0, a:a + n, :].rearrange("p k n -> p (k n)"), W[h][:, 0:n * P], ACT.Copy,
                                   scale=UP).then_inc(w2T_hi, 1)

            def send(n, r, i):
                act.wait_ge(down_full, NSH + n + 1)
                act.wait_ge(rt_in[r], 16 * (i + 1))
                for a in range(2):
                    ins = act.activation(y[:, r, a, :], O[r % 2][:, a * P:(a + 1) * P], ACT.Copy,
                                         scale=rows[:, r, a, P:P + 1])
                ins.then_inc(y_ready, 1)

            def body(u, n, r, i, shared):
                act.wait_ge(gu_full, u + 1)
                if not (isinstance(u, int) and u < 2):
                    act.wait_ge(hid_done, u - 1)
                act.activation(th[:, r % 2, :], S[r % 2][:, 0:2 * UNIT], ACT.Tanh, scale=0.5 / UP ** 2)\
                    .then_inc(gate_tanh, 1)
                if not (isinstance(u, int) and u < 1):
                    high_half(u - 1, r - 1)
                if shared and isinstance(n, int):
                    split_weights(n + 1)
                if not shared and not (isinstance(n, int) and n < 3):
                    send(n - 3, (r - 3) % NRING, i if r >= 3 else i - 1)

            def high_half(u, r):
                act.wait_ge(hid_done, u + 1)
                if not (isinstance(u, int) and u < 2):
                    act.wait_ge(down_full, u - 1)
                act.copy(hid16[:, r % 2, 0, :], hid[:, r % 2, :]).then_inc(hi_done, 1)

            split_weights(0)
            over_units(act, body)
            high_half(NSH + NRT - 1, NRING - 1)
            for n in range(NRT - 3, NRT):
                send(n, n % NRING, n // NRING)

            def finish(b, r, i):
                act.wait_ge(shift_done, b + 1)
                if not (isinstance(b, int) and b < 2):
                    act.wait_ge(res_out[r % 2], 16 * (2 * i + (0 if r < 2 else 1)))
                for t in range(NT):
                    src = acc[:, bass.ds(NT * b + t, 1), :].rearrange("p o d -> p (o d)")
                    ins = act.activation(res[:, r % 2, t, :], src, ACT.Identity, scale=rstd2[:, r, t:t + 1],
                                         bias=shift2[:, r, t:t + 1])
                ins.then_inc(res_done, 1)
            act.sem_inc(res_done, RES_AHEAD)
            over_results(act, finish, 0)

        @block2.vector
        def _(dve):
            count = [0]
            base = [0]

            def chain(ins):
                ins.then_inc(stats_step, 1)
                count[0] += 1
                dve.wait_ge(stats_step, base[0] + count[0])

            def split_weights(e):
                for h, (a, n) in enumerate(((0, 4), (4, 2))):
                    dve.wait_ge(w2T_hi, 2 * e + h + 1)
                    dve.scalar_tensor_tensor(out=w_T[:, place(e), 1, a:a + n, :].rearrange("p k n -> p (k n)"), in0=W[h][:, 0:n * P],
                                             scalar=UP, in1=w_T[:, place(e), 0, a:a + n, :].rearrange("p k n -> p (k n)"),
                                             op0=ALU.mult, op1=ALU.subtract).then_inc(w2T_lo, 1)

            def copy_xT(n, r):
                dve.wait_ge(xT2_full, n + 1)
                if not (isinstance(n, int) and n < 2):
                    dve.wait_ge(gu_full, NSH + n - 1)
                dve.tensor_copy(xT_rt[:, r % 2].rearrange("p s m -> p (s m)"), W[r % 2][:, 0:UNIT].bitcast(FP16))\
                    .then_inc(xT2_read, 1)

            def add_shared(n, r):
                dve.wait_ge(down_full, n + 1)
                dst = acc[:, bass.ds(2 * n, 2), :] if not isinstance(n, int) else acc[:, 2 * n:2 * n + 2, :]
                dve.scalar_tensor_tensor(out=dst.rearrange("p a d -> p (a d)"), in0=O[r % 2][:, 0:UNIT],
                                         scalar=1.0 / (UP * H_UP), in1=x1_in[:, r].rearrange("p a d -> p (a d)"),
                                         op0=ALU.mult, op1=ALU.add).then_inc(acc_done, 1)

            def body(u, n, r, i, shared):
                par = r % 2
                peeled = isinstance(n, int)
                if not shared and peeled and n == 0:
                    copy_xT(0, 0)
                if not shared and not (peeled and n == NRT - 1):
                    copy_xT(n + 1, r + 1)
                dve.wait_ge(gate_tanh, u + 1)
                dve.scalar_tensor_tensor(out=gated[:, par, :], in0=th[:, par, :], scalar=1.0, in1=S[par][:, 0:2 * UNIT],
                                         op0=ALU.add, op1=ALU.mult).then_inc(gated_done, 1)
                if shared and not (peeled and n < 3):
                    add_shared(n - 3, (r - 3) % NRING)
                if not shared and peeled and n < 3:
                    add_shared(NSH - 3 + n, (r - 3) % NRING)
                if not (isinstance(u, int) and u < 1):
                    low_half(u - 1, 1 - par)
                dve.wait_ge(gated_done, u + 1)
                dve.scalar_tensor_tensor(out=hid[:, par, :], in0=gated[:, par, :], scalar=0.5 * H_UP / UP ** 4,
                                         in1=S[par][:, 2 * UNIT:4 * UNIT], op0=ALU.mult, op1=ALU.mult)\
                    .then_inc(hid_done, 1)
                if shared and peeled:
                    split_weights(n + 1)

            def low_half(u, par):
                dve.wait_ge(hi_done, u + 1)
                dve.tensor_tensor(hid16[:, par, 1, :], hid[:, par, :], hid16[:, par, 0, :], ALU.subtract)\
                    .then_inc(lo_done, 1)

            split_weights(0)
            for e in range(NE):
                ins = dve.tensor_scalar(sch["count"][:, e:e + 1], next_slot[:, e:e + 1], float(UNIT - 1 - e * CAP), None,
                                        ALU.add)
            chain(ins)
            chain(dve.tensor_copy(sch_i[:, :], sch["count"][:, :]))
            chain(dve.tensor_scalar(sch_i[:, :], sch_i[:, :], UNIT.bit_length() - 1, None, ALU.logical_shift_right))
            dve.tensor_copy(sch["units"][:, :], sch_i[:, :]).then_inc(units_done, 1)
            over_units(dve, body)
            low_half(NSH + NRT - 1, (NRING - 1) % 2)

            def finish(b, r, i):
                def batch(n):
                    return acc[:, bass.ds(NT * n, NT), :]

                if there(b):
                    dve.wait_ge(zsum_done, b + 1)
                    dve.tensor_tensor(batch(b), batch(b), z[:, r, 0], ALU.add).then_inc(tot_done, 1)
                if there(b - 1):
                    c = (r - 1) % ZRING
                    dve.wait_ge(stats2_done, b)
                    dve.sem_inc(parted, 1)
                    for t in range(NT):
                        ins = dve.bn_aggr(meanvar2[:, c, t, :], stats2[:, c % 2, t, :])
                    ins.then_inc(aggr_done, 1)
                if there(b):
                    dve.wait_ge(tot_done, b + 1)
                    dve.sem_inc(parted, 1)
                    for t in range(NT):
                        src = acc[:, bass.ds(NT * b + t, 1), :].rearrange("p o d -> p (o d)")
                        ins = dve.bn_stats(stats2[:, r % 2, t, :], src)
                    ins.then_inc(stats2_done, 1)
                if there(b - 1):
                    dve.wait_ge(aggr_done, b)
                    dve.tensor_scalar(vareps2[:, c, :], meanvar2[:, c, :, 1], EPS, None, ALU.add).then_inc(var2_done, 1)
                if there(b - 3):
                    c = (r - 3) % ZRING
                    dve.wait_ge(rstd2_done, b - 2)
                    dve.scalar_tensor_tensor(out=shift2[:, c, :], in0=meanvar2[:, c, :, 0], scalar=-1.0,
                                             in1=rstd2[:, c, :], op0=ALU.mult, op1=ALU.mult).then_inc(shift_done, 1)
            over_results(dve, finish, 3)


_INS = ["L0_attn_x", "L0_attn_W1_q", "L0_attn_W2_q", "L0_attn_W1_k", "L0_attn_W2_k", "L0_attn_Wv", "L0_attn_bv",
        "L0_attn_Wo", "L0_attn_bo", "L0_ffn_Wg_s", "L0_ffn_Wu_s", "L0_ffn_Wd_s", "L0_ffn_Wg", "L0_ffn_Wu",
        "L0_ffn_Wd", "L0_ffn_Wr", "L0_ffn_rb"]


def kernel(**inputs):
    import numpy as np
    import concourse.bacc as bacc
    from concourse.bass_utils import run_bass_kernel_spmd

    nc = bacc.Bacc("TRN2", target_bir_lowering=False, num_devices=1)
    arrays, args = {}, []
    for name in _INS:
        a = np.ascontiguousarray(inputs[name])
        arrays[f"in_{name}"] = a
        args.append(nc.dram_tensor(f"in_{name}", a.shape, mybir.dt.from_np(a.dtype), kind="ExternalInput").ap())
    shape = inputs["L0_attn_x"].shape
    out = nc.dram_tensor("out_0", shape, FP32, kind="ExternalOutput").ap()
    block_program(nc, *args, out)
    return run_bass_kernel_spmd(nc, [arrays], core_ids=[0]).results[0]["out_0"]
```
